# Optimizing a Trainium2 kernel written in Bass

```python
import numpy as np
import jax
import jax.numpy as jnp

def _softmax(x, axis=-1):
    return jax.nn.softmax(x, axis=axis)

def _gelu(x):
    return jax.nn.gelu(x, approximate=True)

def _silu(x):
    return jax.nn.silu(x)

def _sigmoid(x):
    return jax.nn.sigmoid(x)

def _layernorm(x, axis=-1, eps=1e-05):
    m = jnp.mean(x, axis=axis, keepdims=True)
    v = jnp.var(x, axis=axis, keepdims=True)
    return (x - m) / jnp.sqrt(v + eps)

def _scatter_add(tgt, idx, src, axis=0):
    return tgt.at[idx].add(src)

def _segment_sum(src, seg, n):
    return jax.ops.segment_sum(src, seg, n)
kernel_name = 'mk_adaln_d1_jaxref_r8_75536b'

def setup_inputs(seed: int=0):
    np.random.seed(seed)
    _w = jnp.asarray

    def _L0_attn_setup():
        import jax, jax.numpy as jnp
        import numpy as np
        B, S, E = (2, 256, 256)
        H, KV, D = (16, 4, 128)
        WIN = 128
        CAP = 50.0
        EPS = 1e-06

        def _rotate_half(x):
            x1, x2 = jnp.split(x, 2, axis=-1)
            return jnp.concatenate([-x2, x1], axis=-1)

        def _rope_tables(seq_len, head_dim):
            half = head_dim // 2
            inv_freq = 1.0 / 10000.0 ** (jnp.arange(0, half, dtype=jnp.float32) / half)
            angles = jnp.outer(jnp.arange(seq_len, dtype=jnp.float32), inv_freq)
            angles = jnp.concatenate([angles, angles], axis=-1)
            return (jnp.cos(angles)[None, :, None, :], jnp.sin(angles)[None, :, None, :])
        key = jax.random.key(seed)
        ks = jax.random.split(key, 5)
        return {'hidden_states': jax.random.normal(ks[0], (B, S, E), jnp.float32), 'wq': 0.02 * jax.random.normal(ks[1], (E, H * D), jnp.float32), 'wk': 0.02 * jax.random.normal(ks[2], (E, KV * D), jnp.float32), 'wv': 0.02 * jax.random.normal(ks[3], (E, KV * D), jnp.float32), 'wo': 0.02 * jax.random.normal(ks[4], (H * D, E), jnp.float32), 'query_scale': jnp.ones((D,), jnp.float32), 'key_scale': jnp.ones((D,), jnp.float32)}
    _L0_attn_in = _L0_attn_setup()

    def _L0_ffn_setup():
        import jax, jax.numpy as jnp
        import numpy as np
        import math
        GOLDEN_CENTER = 1.0 / math.e
        GOLDEN_LOWER = 0.5 - math.log(4.0 / 3.0)
        GOLDEN_UPPER = 0.5
        B, T, D = (4, 128, 256)
        E = 8
        F = 1024 // (E // 2)
        R = 64
        NL = 2

        def _router_weights(x, Wr, temperature):
            logits = jnp.einsum('btd,de->bte', x, Wr)
            inhibition = jax.nn.sigmoid(logits / temperature)
            in_zone = (inhibition >= GOLDEN_LOWER) & (inhibition <= GOLDEN_UPPER)
            distance = jnp.abs(inhibition - GOLDEN_CENTER)
            w = jnp.exp(-distance / 0.1) * in_zone.astype(x.dtype)
            wsum = w.sum(axis=-1, keepdims=True)
            no_expert = wsum < 1e-08
            fb = jnp.exp(-distance / 0.3)
            _, top2 = jax.lax.top_k(fb, 2)
            fb_mask = jax.nn.one_hot(top2, E, dtype=x.dtype).sum(axis=-2)
            fb_w = fb * fb_mask
            fb_w = fb_w / jnp.clip(fb_w.sum(axis=-1, keepdims=True), 1e-08)
            w = jnp.where(no_expert, fb_w, w)
            return w / jnp.clip(w.sum(axis=-1, keepdims=True), 1e-08)
        key = jax.random.key(seed)
        ks = jax.random.split(key, 13)
        s = 0.02
        x = jax.random.normal(ks[0], (B, T, D), dtype=jnp.float32)
        Wg = jax.random.normal(ks[1], (E, D, F), dtype=jnp.float32) * s
        Wu = jax.random.normal(ks[2], (E, D, F), dtype=jnp.float32) * s
        Wd = jax.random.normal(ks[3], (E, F, D), dtype=jnp.float32) * s
        Ga = jax.random.normal(ks[4], (NL, D, R), dtype=jnp.float32) * s
        Gb = jax.random.normal(ks[5], (NL, R, F), dtype=jnp.float32) * s
        Ua = jax.random.normal(ks[6], (NL, D, R), dtype=jnp.float32) * s
        Ub = jax.random.normal(ks[7], (NL, R, F), dtype=jnp.float32) * s
        Da = jax.random.normal(ks[8], (NL, F, R), dtype=jnp.float32) * s
        Db = jax.random.normal(ks[9], (NL, R, D), dtype=jnp.float32) * s
        Wr = jax.random.normal(ks[10], (D, E), dtype=jnp.float32) * s
        temperature = jnp.ones((1,), dtype=jnp.float32)
        return {'x': x, 'Wg': Wg, 'Wu': Wu, 'Wd': Wd, 'Ga': Ga, 'Gb': Gb, 'Ua': Ua, 'Ub': Ub, 'Da': Da, 'Db': Db, 'Wr': Wr, 'temperature': temperature}
    _L0_ffn_in = _L0_ffn_setup()
    _L0_c = _w((lambda *s: np.random.randn(*s).astype(np.float32) * 0.05)(8, 256))
    _L0_wmod = _w((lambda *s: np.random.randn(*s).astype(np.float32) * 0.05)(256, 6 * 256) * 256 ** (-0.5))
    _d = {'L0_attn_hidden_states': _L0_attn_in['hidden_states'], 'L0_attn_wq': _L0_attn_in['wq'], 'L0_attn_wk': _L0_attn_in['wk'], 'L0_attn_wv': _L0_attn_in['wv'], 'L0_attn_wo': _L0_attn_in['wo'], 'L0_attn_query_scale': _L0_attn_in['query_scale'], 'L0_attn_key_scale': _L0_attn_in['key_scale'], 'L0_ffn_Wg': _L0_ffn_in['Wg'], 'L0_ffn_Wu': _L0_ffn_in['Wu'], 'L0_ffn_Wd': _L0_ffn_in['Wd'], 'L0_ffn_Ga': _L0_ffn_in['Ga'], 'L0_ffn_Gb': _L0_ffn_in['Gb'], 'L0_ffn_Ua': _L0_ffn_in['Ua'], 'L0_ffn_Ub': _L0_ffn_in['Ub'], 'L0_ffn_Da': _L0_ffn_in['Da'], 'L0_ffn_Db': _L0_ffn_in['Db'], 'L0_ffn_Wr': _L0_ffn_in['Wr'], 'L0_ffn_temperature': _L0_ffn_in['temperature'], 'L0_c': _L0_c, 'L0_wmod': _L0_wmod}
    _x0 = _d['L0_attn_hidden_states']
    _d['L0_attn_hidden_states'] = jax.random.normal(jax.random.fold_in(jax.random.key(seed), 1), (8, 256, 256), dtype=_x0.dtype)
    del _x0
    return _d

def reference(L0_attn_hidden_states, L0_attn_wq, L0_attn_wk, L0_attn_wv, L0_attn_wo, L0_attn_query_scale, L0_attn_key_scale, L0_ffn_Wg, L0_ffn_Wu, L0_ffn_Wd, L0_ffn_Ga, L0_ffn_Gb, L0_ffn_Ua, L0_ffn_Ub, L0_ffn_Da, L0_ffn_Db, L0_ffn_Wr, L0_ffn_temperature, L0_c, L0_wmod):

    def _L0_attn_ref(hidden_states, wq, wk, wv, wo, query_scale, key_scale):
        import jax, jax.numpy as jnp
        import numpy as np
        B, S, E = (2, 256, 256)
        H, KV, D = (16, 4, 128)
        WIN = 128
        CAP = 50.0
        EPS = 1e-06

        def _rotate_half(x):
            x1, x2 = jnp.split(x, 2, axis=-1)
            return jnp.concatenate([-x2, x1], axis=-1)

        def _rope_tables(seq_len, head_dim):
            half = head_dim // 2
            inv_freq = 1.0 / 10000.0 ** (jnp.arange(0, half, dtype=jnp.float32) / half)
            angles = jnp.outer(jnp.arange(seq_len, dtype=jnp.float32), inv_freq)
            angles = jnp.concatenate([angles, angles], axis=-1)
            return (jnp.cos(angles)[None, :, None, :], jnp.sin(angles)[None, :, None, :])
        b, s, e = hidden_states.shape
        q = (hidden_states @ wq).reshape(b, s, H, D)
        k = (hidden_states @ wk).reshape(b, s, KV, D)
        v = (hidden_states @ wv).reshape(b, s, KV, D)
        cos, sin = _rope_tables(s, D)
        q = q * cos + _rotate_half(q) * sin
        k = k * cos + _rotate_half(k) * sin
        q = q / (jnp.linalg.norm(q, axis=-1, keepdims=True) + EPS) * query_scale
        k = k / (jnp.linalg.norm(k, axis=-1, keepdims=True) + EPS) * key_scale
        k = jnp.repeat(k, H // KV, axis=2)
        v = jnp.repeat(v, H // KV, axis=2)
        scale = 1.0 / np.sqrt(D).astype(np.float32)
        scores = jnp.einsum('bqhd,bkhd->bhqk', q, k) * scale
        scores = jnp.tanh(scores / CAP) * CAP
        pos = jnp.arange(s)
        win_mask = jnp.abs(pos[:, None] - pos[None, :]) <= WIN
        scores = jnp.where(win_mask[None, None], scores, -jnp.inf)
        attn = jax.nn.softmax(scores, axis=-1)
        out = jnp.einsum('bhqk,bkhd->bqhd', attn, v).reshape(b, s, H * D)
        return out @ wo

    def _L0_ffn_ref(x, Wg, Wu, Wd, Ga, Gb, Ua, Ub, Da, Db, Wr, temperature):
        import jax, jax.numpy as jnp
        import numpy as np
        import math
        GOLDEN_CENTER = 1.0 / math.e
        GOLDEN_LOWER = 0.5 - math.log(4.0 / 3.0)
        GOLDEN_UPPER = 0.5
        B, T, D = (4, 128, 256)
        E = 8
        F = 1024 // (E // 2)
        R = 64
        NL = 2

        def _router_weights(x, Wr, temperature):
            logits = jnp.einsum('btd,de->bte', x, Wr)
            inhibition = jax.nn.sigmoid(logits / temperature)
            in_zone = (inhibition >= GOLDEN_LOWER) & (inhibition <= GOLDEN_UPPER)
            distance = jnp.abs(inhibition - GOLDEN_CENTER)
            w = jnp.exp(-distance / 0.1) * in_zone.astype(x.dtype)
            wsum = w.sum(axis=-1, keepdims=True)
            no_expert = wsum < 1e-08
            fb = jnp.exp(-distance / 0.3)
            _, top2 = jax.lax.top_k(fb, 2)
            fb_mask = jax.nn.one_hot(top2, E, dtype=x.dtype).sum(axis=-2)
            fb_w = fb * fb_mask
            fb_w = fb_w / jnp.clip(fb_w.sum(axis=-1, keepdims=True), 1e-08)
            w = jnp.where(no_expert, fb_w, w)
            return w / jnp.clip(w.sum(axis=-1, keepdims=True), 1e-08)
        weights = _router_weights(x, Wr, temperature)
        gate = jnp.einsum('btd,edf->ebtf', x, Wg)
        up = jnp.einsum('btd,edf->ebtf', x, Wu)
        gate = gate.at[:NL].add(jnp.einsum('btd,edr,erf->ebtf', x, Ga, Gb))
        up = up.at[:NL].add(jnp.einsum('btd,edr,erf->ebtf', x, Ua, Ub))
        mid = jax.nn.silu(gate) * up
        out = jnp.einsum('ebtf,efd->ebtd', mid, Wd)
        out = out.at[:NL].add(jnp.einsum('ebtf,efr,erd->ebtd', mid[:NL], Da, Db))
        return jnp.einsum('bte,ebtd->btd', weights, out)
    x = L0_attn_hidden_states
    mod = (_silu(L0_c) @ L0_wmod).reshape(L0_c.shape[0], 6, 1, -1)
    sa, ca, ga, sb, cb, gb = (mod[:, 0], mod[:, 1], mod[:, 2], mod[:, 3], mod[:, 4], mod[:, 5])
    ga = (2 * (ga >= 0) - 1) * jnp.maximum(jnp.abs(ga), 0.25)
    gb = (2 * (gb >= 0) - 1) * jnp.maximum(jnp.abs(gb), 0.25)
    h = _layernorm(x, axis=-1) * (1 + ca) + sa
    x = x + ga * _L0_attn_ref(h, L0_attn_wq, L0_attn_wk, L0_attn_wv, L0_attn_wo, L0_attn_query_scale, L0_attn_key_scale)
    h = _layernorm(x, axis=-1) * (1 + cb) + sb
    x = x + gb * _L0_ffn_ref(h, L0_ffn_Wg, L0_ffn_Wu, L0_ffn_Wd, L0_ffn_Ga, L0_ffn_Gb, L0_ffn_Ua, L0_ffn_Ub, L0_ffn_Da, L0_ffn_Db, L0_ffn_Wr, L0_ffn_temperature)
    return x

_drawn_inputs = setup_inputs


def setup_inputs(seed=0):
    import zlib

    import numpy as np

    out = dict(_drawn_inputs(seed))
    spreads = {'L0_attn_query_scale': (1.0, 0.6), 'L0_attn_key_scale': (1.0, 0.6)}
    factors = {'L0_attn_wq': 8.0,
     'L0_attn_wk': 8.0,
     'L0_attn_wv': 8.0,
     'L0_attn_wo': 8.0,
     'L0_ffn_Wg': 8.0,
     'L0_ffn_Wu': 8.0,
     'L0_ffn_Wd': 8.0,
     'L0_ffn_Ga': 8.0,
     'L0_ffn_Gb': 8.0,
     'L0_ffn_Ua': 8.0,
     'L0_ffn_Ub': 8.0,
     'L0_ffn_Da': 8.0,
     'L0_ffn_Db': 8.0,
     'L0_ffn_Wr': 8.0,
     'L0_c': 8.0,
     'L0_wmod': 8.0}
    for name, (base, spread) in spreads.items():
        noise = np.random.default_rng([zlib.crc32(name.encode()), seed]).standard_normal(out[name].shape)
        drawn = base * np.exp(spread * noise) if base else spread * noise
        out[name] = jnp.asarray(drawn.astype(out[name].dtype))
    for name, factor in factors.items():
        out[name] = (out[name] * factor).astype(out[name].dtype)
    return out
```

```python
from contextlib import ExitStack

import numpy as np

import concourse.bass as bass
from concourse import mybir

F32 = mybir.dt.float32
F32R = mybir.dt.float32r
ALU = mybir.AluOpType
ACT = mybir.ActivationFunctionType
AX_X = mybir.AxisListType.X

P = 128
B, S, E = 8, 256, 256
H, KV, D = 16, 4, 128
G = H // KV
WIN, CAP, EPS = 128, 50.0, 1e-6
LN_EPS = 1e-5
NE, F, R, NL = 8, 256, 64, 2
TT = S // P
KT = E // P
NT = B * TT
SLOTS = H // 2
QKV = (2 * KV + H) * D
CHUNK = 512
CHUNKS = QKV // CHUNK
CENTER = 1.0 / np.e
LOWER, UPPER = 0.5 - float(np.log(4.0 / 3.0)), 0.5
SCALE = 1.0 / float(np.sqrt(D)) / CAP

WK, WQ, WV = 0, (1, 2, 4, 5), 3

PROJ = [("k", 0, 0), ("k", 0, 1), ("q", 0, 0), ("q", 0, 1), ("q", 1, 0),
        ("v", 0, 0), ("v", 0, 1), ("q", 1, 1), ("q", 2, 0), ("q", 2, 1), ("q", 3, 0), ("q", 3, 1)]
LEAD = 5
NP = len(PROJ)
ROT = [u for u in PROJ if u[0] != "v"]
NR = len(ROT)
RING = 5
SLOT_PROJ = [[5, 6, 7], [8], [9], [10], [11], [NP, NP + 1], [NP + 2, NP + 3], [NP + 4]]
SLOT_TURN = [[4], [5], [6], [7], [8], [9], [], [NR, NR + 1, NR + 2, NR + 3]]


def rot_of(p):
    return p if p < 5 else p - 2


def build(nc, a, out):
    ctx = ExitStack()
    stage_a = ExitStack()

    def sb(name, shape, dt=F32, stack=ctx):
        return stack.enter_context(nc.sbuf_tensor(name, shape, dt))

    def ps(name, shape, stack=ctx):
        return stack.enter_context(nc.psum_tensor(name, shape, F32))

    def sem(name):
        return ctx.enter_context(nc.semaphore(name))

    with ctx:
        x_all = sb("x_all", [P, NT, E])
        modc = sb("modc", [P, B, 8])
        gates = sb("gates", [P, B, 2, E])
        ident = sb("ident", [P, P])
        powers = sb("powers", [P, 12])
        raw_e = sb("raw_e", [P, 2, 6, F])

        def sba(name, shape, dt=F32):
            return sb(name, shape, dt, stage_a)

        w_hi = sba("w_hi", [P, CHUNKS, KT, CHUNK], F32R)
        w_lo = sba("w_lo", [P, CHUNKS, KT, CHUNK], F32R)
        wo_hi = sba("wo_hi", [P, H, E], F32R)
        wo_lo = sba("wo_lo", [P, H, E], F32R)
        cosT = sba("cosT", [P, TT, D])
        sinT = sba("sinT", [P, TT, D])
        mask = sba("mask", [P, 2, 2, P])
        kcol = sba("kcol", [P, 1])
        curmod = sba("curmod", [P, 4])
        stats = sba("stats", [P, TT, 6])
        mv = sba("mv", [P, TT, 2])
        veps = sba("veps", [P, TT])
        rstd = sba("rstd", [P, TT])
        xn = sba("xn", [P, TT, E])
        hf = sba("hf", [P, KT, S])
        h_hi = sba("h_hi", [P, KT, S], F32R)
        h_lo = sba("h_lo", [P, KT, S], F32R)
        sq = sba("sq", [P, 4, D])
        prod_c = sba("prod_c", [P, 2, 4, D])
        prod_s = sba("prod_s", [P, 2, 4, D])
        ssq = sba("ssq", [P, 2, 4])
        root = sba("root", [P, 2, 4])
        roote = sba("roote", [P, 2, 4])
        rnorm = sba("rnorm", [P, 2, 4])
        rows = sba("rows", [P, RING, 4, D])
        kf = sba("kf", [P, KV, P])
        kT_hi = sba("kT_hi", [P, TT, KV, P], F32R)
        kT_lo = sba("kT_lo", [P, TT, KV, P], F32R)
        qT_hi = sba("qT_hi", [P, 2, G, S], F32R)
        qT_lo = sba("qT_lo", [P, 2, G, S], F32R)
        vaug = sba("vaug", [P, TT, KV, D + 1])
        probs = sba("probs", [P, 2, 2 * 2 * S])
        rden = sba("rden", [P, TT, 2])
        o_rows = sba("o_rows", [P, TT, 2, D])
        oT_hi = sba("oT_hi", [P, TT, 2, P], F32R)
        oT_lo = sba("oT_lo", [P, TT, 2, P], F32R)
        ygated = sba("ygated", [P, TT, E])

        qks = sba("qks", [P, 2])

        raw_w = probs[:].rearrange("p a (k n) -> p a k n", k=KT)
        cT = kf[:, 0, 0:KT * B].rearrange("p (k b) -> p k b", k=KT)
        scT = kf[:, 1, 0:KT * B].rearrange("p (k b) -> p k b", k=KT)
        wmod_sb = x_all[:, TT:TT + 6 * KT, :].rearrange("p (k j) e -> p k (j e)", k=KT)
        spare = raw_e[:].rearrange("p a m f -> p (a m f)")
        grow, gabs, gsgn, gfin = (spare[0:B, n * 2 * E:(n + 1) * 2 * E] for n in range(4))
        sel = spare[0:B, 8 * E:8 * E + B * P].rearrange("b (c p) -> b c p", c=B)
        stage_a.close()

        h2_hi = sb("h2_hi", [P, KT, NT * P], F32R)
        h2_lo = sb("h2_lo", [P, KT, NT * P], F32R)
        h2f = sb("h2f", [P, 2, KT, 2 * S])
        x2n = sb("x2n", [P, 4, E])
        stats2 = sb("stats2", [P, 4, 6])
        mv2 = sb("mv2", [P, 4, 2])
        veps2 = sb("veps2", [P, 4])
        rstd2 = sb("rstd2", [P, 4])
        wr = sb("wr", [P, KT, NE])
        lowA = sb("lowA", [R, NL, 3, E])
        lowB = sb("lowB", [R, NL, 3, E])
        we_hi = sb("we_hi", [P, 2, 6, F], F32R)
        we_lo = sb("we_lo", [P, 2, 6, F], F32R)
        we_f = sb("we_f", [P, NL, 6, F])
        temp = sb("temp", [P, 1])
        tri = sb("tri", [P, NE, NE])
        r_a = sb("r_a", [P, NT, NE])
        r_b = sb("r_b", [P, NT, NE])
        r_c = sb("r_c", [P, NT, NE])
        r_w = sb("r_w", [P, NT, NE])
        r_fb = sb("r_fb", [P, NT, NE])
        r_wf = sb("r_wf", [P, NT, NE])
        r_gt = sb("r_gt", [P, NT, NE, NE])
        r_eq = sb("r_eq", [P, NT, NE, NE])
        r_s = sb("r_s", [P, 8, NT])
        wcol = sb("wcol", [P, 2, NT])
        silu = sb("silu", [P, 2, 2 * S])
        mid = sb("mid", [P, 2, 2 * S])
        mid_hi = sb("mid_hi", [P, 2, 2, 2 * S], F32R)
        mid_lo = sb("mid_lo", [P, 2, 2, 2 * S], F32R)
        acc = sb("acc", [P, NT, E])

        psum_a = ExitStack()
        ps_proj = ps("ps_proj", [P, 2, 512], psum_a)
        ps_turn = ps("ps_turn", [P, 512], psum_a)
        ps_s = ps("ps_s", [P, 2, 512], psum_a)
        ps_o = ps("ps_o", [P, 2, 512], psum_a)
        ps_y = ps("ps_y", [P, 512], psum_a)
        psum_a.close()
        ps_g = ps("ps_g", [P, 2, 512])
        ps_u = ps("ps_u", [P, 2, 512])
        ps_d = ps("ps_d", [P, 2, 512])
        ps_t = ps("ps_t", [P, 2, 512])

        x_in = [sem("x_first"), sem("x_rest")]
        raw_in = [sem("raw_in0"), sem("raw_in1")]
        expert_in = [sem("expert_in0"), sem("expert_in1")]
        consts = sem("consts")
        wmod_in = sem("wmod_in")
        wo_in = sem("wo_in")
        low_in = sem("low_in")
        out_done = sem("out_done")
        silu_c = sem("silu_c")
        mod_cols = sem("mod_cols")
        mod_rows = sem("mod_rows")
        gate_rows = sem("gate_rows")
        gate_bcast = sem("gate_bcast")
        prep = sem("prep")
        prologue_done = sem("prologue_done")
        w_hi_done = sem("w_hi_done")
        w_lo_done = sem("w_lo_done")
        wo_hi_done = sem("wo_hi_done")
        wo_lo_done = sem("wo_lo_done")
        ln_dve = sem("ln_dve")
        ln_rstd = sem("ln_rstd")
        ln_done = sem("ln_done")
        h_turned = sem("h_turned")
        h_done = sem("h_done")
        h_hi_done = sem("h_hi_done")
        h_split = sem("h_split")
        proj_ready = sem("proj_ready")
        square_ready = sem("square_ready")
        rotated = sem("rotated")
        ssq_ready = sem("ssq_ready")
        root_ready = sem("root_ready")
        rnorm_ready = sem("rnorm_ready")
        rot_sum = sem("rot_sum")
        rows_ready = sem("rows_ready")
        rope_turned = sem("rope_turned")
        k_scaled = sem("k_scaled")
        rope_hi = sem("rope_hi")
        rope_split = sem("rope_split")
        v_ready = sem("v_ready")
        scores_ready = sem("scores_ready")
        tanh_done = sem("tanh_done")
        exp_done = sem("exp_done")
        masked = sem("masked")
        pv_ready = sem("pv_ready")
        rden_done = sem("rden_done")
        o_rows_ready = sem("o_rows_ready")
        o_turned = sem("o_turned")
        o_hi = sem("o_hi")
        o_split = sem("o_split")
        y_ready = sem("y_ready")
        y_gated = sem("y_gated")
        x_updated = sem("x_updated")
        eps_added = sem("eps_added")
        veps_done = sem("veps_done")
        h_mod = sem("h_mod")
        mod_ready = sem("mod_ready")
        curmod_ready = sem("curmod_ready")
        ln2_dve = sem("ln2_dve")
        ln2_rstd = sem("ln2_rstd")
        ln2_veps = sem("ln2_veps")
        ln2_done = sem("ln2_done")
        h2_turned = sem("h2_turned")
        h2_mod = sem("h2_mod")
        h2_hi_done = sem("h2_hi_done")
        h2_split = sem("h2_split")
        logits_ready = sem("logits_ready")
        router_act = sem("router_act")
        router = sem("router")
        low_ready = sem("low_ready")
        we_added = sem("we_added")
        we_hi_done = sem("we_hi_done")
        we_split = sem("we_split")
        gu_ready = sem("gu_ready")
        silu_done = sem("silu_done")
        mid_done = sem("mid_done")
        mid_hi_done = sem("mid_hi_done")
        mid_split = sem("mid_split")
        down_ready = sem("down_ready")
        acc_done = sem("acc_done")
        wcol_ready = sem("wcol_ready")
        final_mul = sem("final_mul")
        final_add = sem("final_add")
        acc_zero = sem("acc_zero")
        stage_a_done = sem("stage_a_done")

        def later(value):
            return not isinstance(value, int) or value > 0

        block = ctx.enter_context(nc.Block())

        @block.sync
        def _(sp):
            sp.dma_start(x_all[:, 0:TT, :], a["x"][:, 0:TT, :]).then_inc(x_in[0], 16)
            sp.dma_start(wmod_sb, a["wmod"]).then_inc(wmod_in, 16)
            for c in range(CHUNKS):
                if c >= 2:
                    sp.wait_ge(w_lo_done, c - 1)
                sp.dma_start(raw_w[:, c % 2], a["wqkv"][:, c]).then_inc(raw_in[c % 2], 16)
            sp.wait_ge(mod_rows, 1)
            sp.dma_start(x_all[:, TT:NT, :], a["x"][:, TT:NT, :]).then_inc(x_in[1], 16)
            for c in range(4):
                sp.wait_ge(w_lo_done, CHUNKS)
                if later(due := c - 1):
                    sp.wait_ge(wo_lo_done, due)
                sp.dma_start(raw_w[:, c % 2].rearrange("p k n -> p (k n)"), a["wo"][:, c]).then_inc(wo_in, 16)
                sp.wait_ge(wo_in, 16 * (c + 1))
            sp.wait_ge(gate_bcast, B)
            for e in range(2):
                sp.dma_start(raw_e[:, e], a["we"][:, e]).then_inc(expert_in[e], 16)
            sp.wait_ge(stage_a_done, 1)
            sp.dma_start(lowA[:], a["lowA"]).then_inc(low_in, 16)
            sp.dma_start(lowB[:], a["lowB"]).then_inc(low_in, 16)
            sp.dma_start(wr[:], a["wr"]).then_inc(low_in, 16)
            sp.dma_start(tri[:], a["tri"]).then_inc(low_in, 16)
            sp.dma_start(temp[:], a["temp"]).then_inc(low_in, 16)

            def load(e, par):
                sp.wait_ge(we_split, 3 * (e - 1))
                sp.dma_start(raw_e[:, par], a["we"][:, e]).then_inc(expert_in[par], 16)
            with sp.Fori(1, NE // 2) as j:
                load(2 * j, 0)
                load(2 * j + 1, 1)
            for n in range(4):
                sp.wait_ge(final_add, n + 1)
                sp.dma_start(out[:, 4 * n:4 * n + 4, :], acc[:, 4 * n:4 * n + 4, :]).then_inc(out_done, 16)
            sp.wait_ge(out_done, 64)

        @block.tensor
        def _(pe):
            def three(dst, hi, lo, w_h, w_l, first, last):
                pe.matmul(dst, hi, w_h, start=first, stop=False, skip_group_check=True)
                pe.matmul(dst, hi, w_l, start=False, stop=False, skip_group_check=True)
                return pe.matmul(dst, lo, w_h, start=False, stop=last, skip_group_check=True)

            pe.wait_ge(silu_c, 1)
            pe.wait_ge(wmod_in, 16)
            for j, block_of in enumerate((0, 1, 3, 4)):
                for et in range(KT):
                    for k in range(KT):
                        lo_ = block_of * E + et * P
                        mm = pe.matmul(ps_s[:, 0, (2 * j + et) * B:(2 * j + et + 1) * B], wmod_sb[:, k, lo_:lo_ + P],
                                       scT[:, k, :], start=(j == 0 and et == 0 and k == 0), stop=(k == KT - 1),
                                       skip_group_check=True)
            mm.then_inc(mod_cols, 1)
            for j, block_of in enumerate((2, 5)):
                for k in range(KT):
                    mm = pe.matmul(ps_s[0:B, 1, j * E:(j + 1) * E], scT[:, k, :],
                                   wmod_sb[:, k, block_of * E:(block_of + 1) * E],
                                   start=(j == 0 and k == 0), stop=(k == KT - 1), skip_group_check=True)
            mm.then_inc(mod_rows, 1)
            pe.wait_ge(gate_rows, 5)
            for b in range(B):
                if later(due := b - 1):
                    pe.wait_ge(gate_bcast, due)
                pe.matmul(ps_o[:, b % 2, :], sel[:, b, :], gfin, start=True, stop=True).then_inc(prep, 1)

            def turn_h(b):
                pe.wait_ge(ln_done, 2 * b + 2)
                for k in range(KT):
                    for t in range(TT):
                        mm = pe.transpose(ps_turn[:, k * S + t * P:k * S + (t + 1) * P], xn[:, t, k * P:(k + 1) * P], ident[:])
                mm.then_inc(h_turned, 1)

            def project(b, p):
                kind, g, t = PROJ[p]
                if p >= 2:
                    before = PROJ[p - 2][0]
                    if before == "v":
                        pe.wait_ge(v_ready, 2 * b + p - 6)
                    else:
                        pe.wait_ge(ssq_ready, NR * b + rot_of(p - 2) + 1)
                else:
                    if later(due := NR * b - 1 + p):
                        pe.wait_ge(ssq_ready, due)
                pe.wait_ge(h_split, b + 1)
                c = WK if kind == "k" else WV if kind == "v" else WQ[g]
                if isinstance(b, int) and b == 0:
                    pe.wait_ge(w_lo_done, c + 1)
                for k in range(KT):
                    mm = three(ps_proj[:, p % 2, :], h_hi[:, k, t * P:(t + 1) * P], h_lo[:, k, t * P:(t + 1) * P],
                               w_hi[:, c, k, :], w_lo[:, c, k, :], k == 0, k == KT - 1)
                mm.then_inc(proj_ready, 1)

            def turn_free(b, r):
                if r == 0:
                    if isinstance(b, int) and b == 0:
                        pe.wait_ge(h_done, 1)
                    else:
                        pe.wait_ge(o_split, SLOTS * b - 1)
                elif r <= 2:
                    pe.wait_ge(k_scaled, 2 * b + r)
                elif r == 3:
                    pe.wait_ge(rope_split, NR * b + 3)
                else:
                    if later(due := SLOTS * b + r - 4):
                        pe.wait_ge(o_split, due)

            def turn_rows(b, r):
                turn_free(b, r)
                pe.wait_ge(rows_ready, NR * b + r + 1)
                for i in range(4):
                    mm = pe.transpose(ps_turn[:, i * P:(i + 1) * P], rows[:, r % RING, i, :], ident[:])
                mm.then_inc(rope_turned, 1)

            def turn_o(b, i, last):
                if i == -1:
                    pe.wait_ge(rope_split, NR * b + 4)
                elif i == 4:
                    pe.wait_ge(rope_split, NR * b + 9)
                    if not last:
                        pe.wait_ge(h_done, b + 2)
                elif i == 6:
                    pe.wait_ge(o_split, SLOTS * b + 6)
                else:
                    pe.wait_ge(rope_split, NR * b + 5 + i)
                pe.wait_ge(o_rows_ready, SLOTS * b + i + 1)
                for t in range(TT):
                    for h in range(2):
                        mm = pe.transpose(ps_turn[:, (2 * t + h) * P:(2 * t + h + 1) * P], o_rows[:, t, h, :], ident[:])
                mm.then_inc(o_turned, 1)

            def out_proj(b, i):
                pe.wait_ge(o_split, SLOTS * b + i + 1)
                pair = i % SLOTS
                if pair == 0:
                    if later(due := b):
                        pe.wait_ge(y_gated, due)
                if isinstance(b, int) and b == 0:
                    pe.wait_ge(wo_lo_done, pair // 2 + 1)
                for t in range(TT):
                    for h in range(2):
                        mm = three(ps_y[:, t * E:(t + 1) * E], oT_hi[:, t, h, :], oT_lo[:, t, h, :],
                                   wo_hi[:, 2 * pair + h, :], wo_lo[:, 2 * pair + h, :],
                                   pair == 0 and t == 0 and h == 0, pair == SLOTS - 1 and h == 1)
                if pair == SLOTS - 1:
                    mm.then_inc(y_ready, 1)

            def scores(b, i):
                g, pair = i // 2, i % 2
                pe.wait_ge(rope_split, NR * b + 4 + 2 * g)
                if later(due := SLOTS * b + i):
                    pe.wait_ge(exp_done, due)
                for t in range(TT):
                    q = slice(2 * pair, 2 * pair + 2)
                    mm = three(ps_s[:, t, :], kT_hi[:, t, g, :], kT_lo[:, t, g, :],
                               qT_hi[:, g % 2, q, :].rearrange("p h s -> p (h s)"),
                               qT_lo[:, g % 2, q, :].rearrange("p h s -> p (h s)"), True, True)
                mm.then_inc(scores_ready, 1)

            def weighted(b, i):
                g = i // 2
                pe.wait_ge(masked, SLOTS * b + i + 1)
                if later(due := SLOTS * b + i):
                    pe.wait_ge(o_rows_ready, due)
                if i == 0:
                    pe.wait_ge(v_ready, 2 * b + 2)
                for t in range(TT):
                    for h in range(2):
                        for k in range(TT):
                            at = (2 * k + h) * S + t * P
                            mm = pe.matmul(ps_o[:, t, h * (D + 1):(h + 1) * (D + 1)], probs[:, i % 2, at:at + P],
                                           vaug[:, k, g, :], start=(h == 0 and k == 0), stop=(k == TT - 1),
                                           skip_group_check=True)
                mm.then_inc(pv_ready, 1)

            def batch(b, first, last):
                for i in range(SLOTS):
                    scores(b, i)
                    if not (first and i == 0):
                        turn_o(b, i - 1, last)
                    for p in SLOT_PROJ[i]:
                        if p < NP:
                            project(b, p)
                        elif not last:
                            project(b + 1, p - NP)
                    turns = SLOT_TURN[i]
                    if i == 7 and not last:
                        turn_rows(b + 1, 0)
                    if not (first and i == 0):
                        out_proj(b, i - 1)
                    if i == 7:
                        if not last:
                            turn_rows(b + 1, 1)
                            turn_rows(b + 1, 2)
                    else:
                        for r in turns:
                            turn_rows(b, r)
                    if i == 4 and not last:
                        pe.wait_ge(rope_split, NR * b + 9)
                        turn_h(b + 1)
                    weighted(b, i)
                    if i == 7 and not last:
                        turn_rows(b + 1, 3)

            turn_h(0)
            for p in range(4):
                project(0, p)
            for r in range(4):
                turn_rows(0, r)
            project(0, 4)
            batch(0, True, False)
            with pe.Fori(1, B - 1) as b:
                batch(b, False, False)
            batch(B - 1, False, True)
            pe.wait_ge(o_split, SLOTS * B - 1)
            pe.wait_ge(o_rows_ready, SLOTS * B)
            for t in range(TT):
                for h in range(2):
                    mm = pe.transpose(ps_turn[:, (2 * t + h) * P:(2 * t + h + 1) * P], o_rows[:, t, h, :], ident[:])
            mm.then_inc(o_turned, 1)
            out_proj(B, -1)

            pe.wait_ge(low_in, 80)
            pe.wait_ge(stage_a_done, 1)
            for e in range(NL):
                for m in range(3):
                    i = 3 * e + m
                    if later(due := i - 1):
                        pe.wait_ge(we_added, due)
                    for k in range(KT):
                        mm = pe.matmul(ps_d[:, i % 2, k * F:(k + 1) * F], lowA[:, e, m, k * P:(k + 1) * P], lowB[:, e, m, :],
                                       start=(k == 0), stop=True, skip_group_check=True)
                    mm.then_inc(low_ready, 1)
            for n in range(4):
                for t in range(4):
                    pe.wait_ge(ln2_done, 4 * n + t + 1)
                if later(due := 4 * n):
                    pe.wait_ge(h2_mod, due)
                for bb in range(2):
                    for k in range(KT):
                        for t in range(TT):
                            mm = pe.transpose(ps_t[:, bb, k * S + t * P:k * S + (t + 1) * P],
                                              x2n[:, 2 * bb + t, k * P:(k + 1) * P], ident[:])
                mm.then_inc(h2_turned, 1)
                pe.wait_ge(h2_mod, 4 * n + 4)
                for t in range(4):
                    for k in range(KT):
                        mm = pe.matmul(ps_u[:, 1, (4 * n + t) * NE:(4 * n + t + 1) * NE], h2f[:, n % 2, k, t * P:(t + 1) * P],
                                       wr[:, k, :], start=(n == 0 and t == 0 and k == 0), stop=(k == KT - 1),
                                       skip_group_check=True)
                mm.then_inc(logits_ready, 1)

            def gate_up(e, par, n):
                m = 4 * e + n
                if n == 0:
                    pe.wait_ge(we_split, 3 * e + 2)
                if isinstance(m, int) and m == 0:
                    pe.wait_ge(router_act, 1)
                if isinstance(e, int) and e == 0:
                    pe.wait_ge(h2_split, n + 1)
                for f in range(2):
                    if later(due := 2 * m + f - 1):
                        pe.wait_ge(mid_done, due)
                    for dst, w0 in ((ps_g, 0), (ps_u, 2)):
                        for k in range(KT):
                            mm = three(dst[:, f, :], we_hi[:, par, w0 + k, f * P:(f + 1) * P],
                                       we_lo[:, par, w0 + k, f * P:(f + 1) * P],
                                       h2_hi[:, k, n * 512:(n + 1) * 512], h2_lo[:, k, n * 512:(n + 1) * 512],
                                       k == 0, k == KT - 1)
                        mm.then_inc(gu_ready, 1)

            def down(e, par, n):
                m = 4 * e + n
                if n == 0:
                    pe.wait_ge(we_split, 3 * e + 3)
                pe.wait_ge(mid_split, 2 * m + 2)
                for half in range(2):
                    if later(due := 4 * m - 2 + 2 * half):
                        pe.wait_ge(acc_done, due)
                    for t in range(2):
                        tt = 2 * half + t
                        for f in range(2):
                            mm = three(ps_d[:, half, t * E:(t + 1) * E], mid_hi[:, n % 2, f, tt * P:(tt + 1) * P],
                                       mid_lo[:, n % 2, f, tt * P:(tt + 1) * P],
                                       we_hi[:, par, 4 + f, :], we_lo[:, par, 4 + f, :], t == 0 and f == 0, f == 1)
                    mm.then_inc(down_ready, 1)

            def pair(j, first):
                for par in range(2):
                    e = 2 * j + par
                    for n in range(4):
                        gate_up(e, par, n)
                        if n:
                            down(e, par, n - 1)
                        elif not (first and par == 0):
                            down(e - 1, 1 - par, 3)

            pair(0, True)
            with pe.Fori(1, NE // 2 - 1) as j:
                pair(j, False)
            pair(NE // 2 - 1, False)
            down(NE - 1, 1, 3)

        @block.scalar
        def _(act):
            act.dma_start(cT, a["cT"]).then_inc(consts, 16)
            act.dma_start(ident[:], a["ident"]).then_inc(consts, 16)
            act.dma_start(powers[:], a["powers"]).then_inc(consts, 16)
            act.dma_start(sel, a["sel"]).then_inc(consts, 16)
            act.dma_start(cosT[:], a["cos"]).then_inc(consts, 16)
            act.dma_start(sinT[:], a["sin"]).then_inc(consts, 16)
            act.dma_start(mask[:], a["mask"]).then_inc(consts, 16)
            act.dma_start(qks[:], a["qks"]).then_inc(consts, 16)
            act.wait_ge(consts, 128)
            act.activation(scT, cT, ACT.Silu).then_inc(silu_c, 1)

            def split_w(c):
                act.wait_ge(raw_in[c % 2], 16 * (c // 2 + 1))
                act.activation(w_hi[:, c], raw_w[:, c % 2], ACT.Copy).then_inc(w_hi_done, 1)

            def modulate(b):
                act.wait_ge(h_turned, b + 1)
                if later(due := b):
                    act.wait_ge(h_hi_done, due)
                if later(due := b):
                    act.wait_ge(h_split, due)
                for k in range(KT):
                    act.activation(hf[:, k, :], ps_turn[:, k * S:(k + 1) * S], ACT.Identity,
                                   bias=curmod[:, k:k + 1], scale=curmod[:, 2 + k:3 + k]).then_inc(h_mod if k < KT - 1 else h_done, 1)
                act.wait_ge(h_mod, b + 1)
                act.wait_ge(h_done, b + 1)
                if later(due := NP * b):
                    act.wait_ge(proj_ready, due)
                act.activation(h_hi[:], hf[:], ACT.Copy).then_inc(h_hi_done, 1)

            def square(b, p):
                act.wait_ge(proj_ready, NP * b + p + 1)
                if PROJ[p][0] == "v":
                    t = PROJ[p][2]
                    if later(due := SLOTS * b):
                        act.wait_ge(pv_ready, due)
                    act.activation(vaug[:, t, :, 0:D], ps_proj[:, p % 2, :].rearrange("p (h d) -> p h d", h=KV),
                                   ACT.Copy).then_inc(v_ready, 1)
                else:
                    if later(due := NR * b + rot_of(p)):
                        act.wait_ge(ssq_ready, due)
                    act.activation(sq[:].rearrange("p h d -> p (h d)"), ps_proj[:, p % 2, :], ACT.Square).then_inc(square_ready, 1)

            def rope_head(b, r):
                kind, g, t = ROT[r]
                act.wait_ge(rope_turned, NR * b + r + 1)
                src = ps_turn[:].rearrange("p (h q) -> p h q", h=4)
                if kind == "k":
                    if r == 1:
                        act.wait_ge(rope_split, NR * b + 1)
                    act.activation(kf[:], src, ACT.Copy, scale=kcol[:, 0:1]).then_inc(k_scaled, 1)
                    act.wait_ge(k_scaled, 2 * b + r + 1)
                    if later(due := SLOTS * b):
                        act.wait_ge(scores_ready, due)
                    act.activation(kT_hi[:, t], kf[:], ACT.Copy).then_inc(rope_hi, 1)
                else:
                    if g >= 2:
                        act.wait_ge(scores_ready, SLOTS * b + 2 * (g - 1))
                    else:
                        if later(due := SLOTS * (b - 1) + 2 * (g + 3)):
                            act.wait_ge(scores_ready, due)
                    act.activation(qT_hi[:, g % 2, :, t * P:(t + 1) * P], src, ACT.Copy).then_inc(rope_hi, 1)

            def soft(b, i):
                act.wait_ge(scores_ready, SLOTS * b + i + 1)
                act.activation(ps_s[:], ps_s[:], ACT.Tanh).then_inc(tanh_done, 1)

            def expo(b, i):
                act.wait_ge(tanh_done, SLOTS * b + i + 1)
                if later(due := SLOTS * b + i - 1):
                    act.wait_ge(pv_ready, due)
                act.activation(probs[:, i % 2, :], ps_s[:].rearrange("p k n -> p (k n)"), ACT.Exp, scale=CAP).then_inc(exp_done, 1)

            def o_head(b, i):
                act.wait_ge(o_turned, SLOTS * b + i + 1)
                act.activation(oT_hi[:].rearrange("p t h q -> p (t h q)"), ps_turn[:], ACT.Copy).then_inc(o_hi, 1)

            def batch(b, first, last):
                for i in range(SLOTS):
                    soft(b, i)
                    if not (first and i == 0):
                        o_head(b, i - 1)
                    expo(b, i)
                    for p in SLOT_PROJ[i]:
                        if p < NP:
                            square(b, p)
                        elif not last:
                            square(b + 1, p - NP)
                    for r in SLOT_TURN[i]:
                        if r < NR:
                            rope_head(b, r)
                        elif not last:
                            rope_head(b + 1, r - NR)
                    if i == 4 and not last:
                        modulate(b + 1)

            act.wait_ge(mod_cols, 1)
            cols = ps_s[:, 0, 0:8 * B].rearrange("p (j b) -> p b j", b=B)
            act.activation(modc[:, :, 0:2], cols[:, :, 0:2], ACT.Copy)
            act.activation(modc[:, :, 4:6], cols[:, :, 4:6], ACT.Copy)
            act.activation(modc[:, :, 2:4], cols[:, :, 2:4], ACT.Copy, bias=1.0)
            act.activation(modc[:, :, 6:8], cols[:, :, 6:8], ACT.Copy, bias=1.0).then_inc(mod_ready, 4)
            for b in range(B):
                act.wait_ge(prep, b + 1)
                act.activation(gates[:, b].rearrange("p a e -> p (a e)"), ps_o[:, b % 2, :], ACT.Copy).then_inc(gate_bcast, 1)
            split_w(0)
            modulate(0)
            for p in range(2):
                square(0, p)
            split_w(1)
            for p in range(2, 4):
                square(0, p)
            for r in range(4):
                rope_head(0, r)
            split_w(2)
            square(0, 4)
            for c in range(3, CHUNKS):
                split_w(c)
            for c in range(4):
                act.wait_ge(wo_in, 16 * (c + 1))
                act.activation(wo_hi[:, 4 * c:4 * c + 4, :].rearrange("p h e -> p (h e)"),
                               raw_w[:, c % 2].rearrange("p k n -> p (k n)"), ACT.Copy).then_inc(wo_hi_done, 1)
            act.wait_ge(wo_lo_done, 4)
            batch(0, True, False)
            with act.Fori(1, B - 1) as b:
                batch(b, False, False)
            batch(B - 1, False, True)
            o_head(B, -1)

            act.wait_ge(stage_a_done, 1)
            for n in range(4):
                act.wait_ge(h2_turned, n + 1)
                if n >= 2:
                    act.wait_ge(h2_split, n - 1)
                    act.wait_ge(logits_ready, n - 1)
                for bb in range(2):
                    for k in range(KT):
                        act.activation(h2f[:, n % 2, k, bb * S:(bb + 1) * S], ps_t[:, bb, k * S:(k + 1) * S], ACT.Identity,
                                       bias=modc[:, 2 * n + bb, 4 + k:5 + k], scale=modc[:, 2 * n + bb, 6 + k:7 + k]).then_inc(h2_mod, 1)
                act.wait_ge(h2_mod, 4 * n + 4)
                act.activation(h2_hi[:, :, n * 512:(n + 1) * 512], h2f[:, n % 2], ACT.Copy).then_inc(h2_hi_done, 1)
            act.wait_ge(router, 3)
            act.activation(r_b[:], r_a[:], ACT.Exp, scale=-1.0).then_inc(router_act, 1)
            act.wait_ge(router, 9)
            act.activation(r_w[:], r_c[:], ACT.Exp, scale=-1.0 / 0.1).then_inc(router_act, 1)
            act.activation(r_fb[:], r_c[:], ACT.Exp, scale=-1.0 / 0.3).then_inc(router_act, 1)

            def split_e(e, par, from_sum):
                for m in range(3):
                    if from_sum:
                        act.wait_ge(we_added, 3 * e + m + 1)
                    else:
                        act.wait_ge(expert_in[par], 8 * e + 16 - 8 * par)
                    if later(due := 16 * (e - 1) if m < 2 else 8 * (e - 1)):
                        act.wait_ge(gu_ready if m < 2 else down_ready, due)
                    src = we_f[:, e, 2 * m:2 * m + 2, :] if from_sum else raw_e[:, par, 2 * m:2 * m + 2, :]
                    act.activation(we_hi[:, par, 2 * m:2 * m + 2, :], src, ACT.Copy).then_inc(we_hi_done, 1)

            def silu_of(m, f):
                act.wait_ge(gu_ready, 4 * m + 2 * f + 1)
                if later(due := 2 * m + f - 1):
                    act.wait_ge(mid_done, due)
                act.activation(silu[:, f, :], ps_g[:, f, :], ACT.Silu).then_inc(silu_done, 1)

            def mid_head(m, f, n):
                act.wait_ge(mid_done, 2 * m + f + 1)
                if later(due := 2 * (m - 1)):
                    act.wait_ge(down_ready, due)
                act.activation(mid_hi[:, n % 2, f, :], mid[:, f, :], ACT.Copy).then_inc(mid_hi_done, 1)

            def pair(j, first, last):
                for par in range(2):
                    e = 2 * j + par
                    for n in range(4):
                        m = 4 * e + n
                        silu_of(m, 0)
                        silu_of(m, 1)
                        mid_head(m, 0, n)
                        mid_head(m, 1, n)
                        if n == 1 and not (first and par == 0) and not (last and par == 1):
                            split_e(e + 1, 1 - par, False)

            split_e(0, 0, True)
            split_e(1, 1, True)
            pair(0, True, False)
            with act.Fori(1, NE // 2 - 1) as j:
                pair(j, False, False)
            pair(NE // 2 - 1, False, True)

        @block.vector
        def _(dve):
            dve.wait_ge(consts, 128)
            dve.scalar_tensor_tensor(kcol[:], qks[:, 0:1], SCALE, qks[:, 1:2], ALU.mult, ALU.mult).then_inc(prologue_done, 1)
            dve.memset(vaug[:, :, :, D:D + 1], 1.0).then_inc(prologue_done, 1)

            def norm_stats(b):
                dve.wait_ge(x_in[0] if isinstance(b, int) and b == 0 else x_in[1], 16)
                if later(due := b):
                    dve.wait_ge(ln_rstd, due)
                for t in range(TT):
                    dve.bn_stats(stats[:, t, :], x_all[:, TT * b + t, :]).then_inc(ln_dve, 1)
                if later(due := b):
                    dve.wait_ge(h_done, due)
                if isinstance(b, int) and b == 0:
                    dve.wait_ge(mod_ready, 4)
                dve.wait_ge(ln_dve, 4 * b + 2)
                dve.tensor_copy(curmod[:], modc[:, b, 0:4]).then_inc(curmod_ready, 1)
                for t in range(TT):
                    dve.bn_aggr(mv[:, t, :], stats[:, t, :]).then_inc(ln_dve, 1)

            def norm_rows(b):
                dve.wait_ge(ln_rstd, b + 1)
                if later(due := b):
                    dve.wait_ge(h_turned, due)
                for t in range(TT):
                    dve.tensor_scalar(xn[:, t, :], x_all[:, TT * b + t, :], mv[:, t, 0:1], rstd[:, t:t + 1],
                                      ALU.subtract, ALU.mult).then_inc(ln_done, 1)

            def split_w(c):
                dve.wait_ge(w_hi_done, c + 1)
                dve.tensor_tensor(w_lo[:, c], raw_w[:, c % 2], w_hi[:, c], ALU.subtract).then_inc(w_lo_done, 1)

            def h_tail(b):
                dve.wait_ge(h_hi_done, b + 1)
                dve.tensor_tensor(h_lo[:], hf[:], h_hi[:], ALU.subtract).then_inc(h_split, 1)

            def rotate(b, p):
                r = rot_of(p)
                t = PROJ[p][2]
                src = ps_proj[:, p % 2, :].rearrange("p (h d) -> p h d", h=4)
                cs = cosT[:, t, :].unsqueeze(1).broadcast_to([P, 4, D])
                dve.wait_ge(square_ready, NR * b + r + 1)
                if later(due := NR * b + r - 1):
                    dve.wait_ge(rows_ready, due)
                dve.tensor_tensor(prod_c[:, r % 2], src, cs, ALU.mult).then_inc(rotated, 1)
                for half in range(2):
                    o = half * D // 2
                    other = D // 2 - o
                    sn = sinT[:, t, o:o + D // 2].unsqueeze(1).broadcast_to([P, 4, D // 2])
                    dve.tensor_tensor(prod_s[:, r % 2, :, o:o + D // 2], src[:, :, other:other + D // 2], sn,
                                      ALU.mult).then_inc(rotated, 1)

            def squares(b, p):
                r = rot_of(p)
                dve.tensor_reduce(ssq[:, r % 2, :], sq[:], AX_X, ALU.add).then_inc(ssq_ready, 1)

            def inverse(b, p):
                r = rot_of(p)
                dve.wait_ge(root_ready, NR * b + r + 1)
                dve.tensor_scalar(roote[:, r % 2, :], root[:, r % 2, :], EPS, None, ALU.add).then_inc(eps_added, 1)
                dve.wait_ge(eps_added, NR * b + r + 1)
                dve.reciprocal(rnorm[:, r % 2, :], roote[:, r % 2, :]).then_inc(rnorm_ready, 1)

            def rope_tail(b, r):
                kind, g, t = ROT[r]
                dve.wait_ge(rope_hi, NR * b + r + 1)
                if kind == "k":
                    dve.tensor_tensor(kT_lo[:, t], kf[:], kT_hi[:, t], ALU.subtract).then_inc(rope_split, 1)
                else:
                    q = slice(t * P, (t + 1) * P)
                    dve.tensor_tensor(qT_lo[:, g % 2, :, q], ps_turn[:].rearrange("p (h q) -> p h q", h=4),
                                      qT_hi[:, g % 2, :, q], ALU.subtract).then_inc(rope_split, 1)

            def apply_mask(b, i):
                dve.wait_ge(exp_done, SLOTS * b + i + 1)
                pm = probs[:, i % 2, P:7 * P].rearrange("p (k s c) -> p k s c", k=2, s=3)[:, :, 0:3:2, :]
                dve.tensor_tensor(pm, pm, mask[:], ALU.mult).then_inc(masked, 1)

            def normalise(b, i):
                dve.wait_ge(pv_ready, SLOTS * b + i + 1)
                o = ps_o[:, :, 0:2 * (D + 1)].rearrange("p t (h d) -> p t h d", h=2)
                dve.reciprocal(rden[:], o[:, :, :, D]).then_inc(rden_done, 1)
                dve.wait_ge(rden_done, SLOTS * b + i + 1)
                if later(due := SLOTS * b + i):
                    dve.wait_ge(o_turned, due)
                dve.tensor_tensor(o_rows[:], o[:, :, :, 0:D], rden[:].unsqueeze(3).broadcast_to([P, TT, 2, D]),
                                  ALU.mult).then_inc(o_rows_ready, 1)

            def o_tail(b, i):
                dve.wait_ge(o_hi, SLOTS * b + i + 1)
                dve.tensor_tensor(oT_lo[:].rearrange("p t h q -> p (t h q)"), ps_turn[:],
                                  oT_hi[:].rearrange("p t h q -> p (t h q)"), ALU.subtract).then_inc(o_split, 1)

            def residual(b):
                dve.wait_ge(y_ready, b + 1)
                if isinstance(b, int) and b == 0:
                    dve.wait_ge(gate_bcast, B)
                ga = gates[:, b, 0, :].unsqueeze(1).broadcast_to([P, TT, E])
                dve.tensor_tensor(ygated[:], ps_y[:].rearrange("p (t e) -> p t e", t=TT), ga, ALU.mult).then_inc(y_gated, 1)
                dve.wait_ge(y_gated, b + 1)
                xb = x_all[:, bass.ds(TT * b, TT), :]
                dve.tensor_tensor(xb, xb, ygated[:], ALU.add).then_inc(x_updated, 1)

            def batch(b, first, last):
                for i in range(SLOTS):
                    if not (first and i == 0):
                        o_tail(b, i - 1)
                    ps_ = [(b, p) if p < NP else (b + 1, p - NP) for p in SLOT_PROJ[i] if p < NP or not last]
                    ps_ = [(bb, p) for bb, p in ps_ if PROJ[p][0] != "v"]
                    apply_mask(b, i)
                    for bb, p in ps_:
                        rotate(bb, p)
                        squares(bb, p)
                        inverse(bb, p)
                    for r in SLOT_TURN[i]:
                        if r < NR:
                            rope_tail(b, r)
                        elif not last and r < NR + 3:
                            rope_tail(b + 1, r - NR)
                    if i == 0 and not first:
                        residual(b - 1)
                    if not last:
                        if i == 1:
                            norm_stats(b + 1)
                        if i == 2:
                            norm_rows(b + 1)
                        if i == 4:
                            h_tail(b + 1)
                    normalise(b, i)
                    if i == 7 and not last:
                        rope_tail(b + 1, 3)

            norm_stats(0)
            norm_rows(0)
            dve.wait_ge(mod_rows, 1)
            dve.tensor_copy(grow, ps_s[0:B, 1, :]).then_inc(gate_rows, 1)
            dve.wait_ge(gate_rows, 1)
            dve.scalar_tensor_tensor(gabs, grow, -1.0, grow, ALU.mult, ALU.max).then_inc(gate_rows, 1)
            dve.tensor_scalar(gsgn, grow, 0.0, 2.0, ALU.is_ge, ALU.mult).then_inc(gate_rows, 1)
            dve.wait_ge(gate_rows, 3)
            dve.tensor_scalar(gsgn, gsgn, -1.0, None, ALU.add).then_inc(gate_rows, 1)
            dve.wait_ge(gate_rows, 4)
            dve.scalar_tensor_tensor(gfin, gabs, 0.25, gsgn, ALU.max, ALU.mult).then_inc(gate_rows, 1)
            split_w(0)
            h_tail(0)
            for p in range(2):
                rotate(0, p)
                squares(0, p)
                inverse(0, p)
            split_w(1)
            for p in range(2, 4):
                rotate(0, p)
                squares(0, p)
                inverse(0, p)
            for r in range(4):
                rope_tail(0, r)
            split_w(2)
            rotate(0, 4)
            squares(0, 4)
            inverse(0, 4)
            for c in range(3, CHUNKS):
                split_w(c)
            for c in range(4):
                dve.wait_ge(wo_hi_done, c + 1)
                sl = slice(4 * c, 4 * c + 4)
                dve.tensor_tensor(wo_lo[:, sl, :].rearrange("p h e -> p (h e)"), raw_w[:, c % 2].rearrange("p k n -> p (k n)"),
                                  wo_hi[:, sl, :].rearrange("p h e -> p (h e)"), ALU.subtract).then_inc(wo_lo_done, 1)
            batch(0, True, False)
            with dve.Fori(1, B - 1) as b:
                batch(b, False, False)
            batch(B - 1, False, True)
            o_tail(B, -1)
            dve.wait_ge(y_ready, B)
            dve.tensor_tensor(ygated[:], ps_y[:].rearrange("p (t e) -> p t e", t=TT),
                              gates[:, B - 1, 0, :].unsqueeze(1).broadcast_to([P, TT, E]), ALU.mult).then_inc(y_gated, 1)
            dve.wait_ge(y_gated, B)
            xb = x_all[:, NT - TT:NT, :]
            dve.tensor_tensor(xb, xb, ygated[:], ALU.add).then_inc(x_updated, 1)
            dve.wait_ge(x_updated, B)
            dve.memset(ygated[:, 0, 0:1], 0.0).then_inc(stage_a_done, 1)

            for n in range(4):
                for t in range(4):
                    if n:
                        dve.wait_ge(ln2_rstd, n)
                    dve.bn_stats(stats2[:, t, :], x_all[:, 4 * n + t, :]).then_inc(ln2_dve, 1)
                for t in range(4):
                    dve.wait_ge(ln2_dve, 8 * n + t + 1)
                    dve.bn_aggr(mv2[:, t, :], stats2[:, t, :]).then_inc(ln2_dve, 1)
                if n:
                    dve.wait_ge(h2_hi_done, n)
                    m = slice((n - 1) * 512, n * 512)
                    dve.tensor_tensor(h2_lo[:, :, m], h2f[:, (n - 1) % 2], h2_hi[:, :, m], ALU.subtract).then_inc(h2_split, 1)
                dve.wait_ge(ln2_rstd, n + 1)
                if later(due := n):
                    dve.wait_ge(h2_turned, due)
                for t in range(4):
                    dve.tensor_scalar(x2n[:, t, :], x_all[:, 4 * n + t, :], mv2[:, t, 0:1], rstd2[:, t:t + 1],
                                      ALU.subtract, ALU.mult).then_inc(ln2_done, 1)
                if n == 0:
                    for e in range(NL):
                        dve.wait_ge(expert_in[e], 16)
                        for m3 in range(3):
                            i = 3 * e + m3
                            dve.wait_ge(low_ready, i + 1)
                            dve.tensor_tensor(we_f[:, e, 2 * m3:2 * m3 + 2, :], ps_d[:, i % 2, :].rearrange("p (k f) -> p k f", k=2),
                                              raw_e[:, e, 2 * m3:2 * m3 + 2, :], ALU.add).then_inc(we_added, 1)
            dve.wait_ge(h2_hi_done, 4)
            dve.tensor_tensor(h2_lo[:, :, 3 * 512:], h2f[:, 1], h2_hi[:, :, 3 * 512:], ALU.subtract).then_inc(h2_split, 1)

            count = [0]

            def step(instruction):
                count[0] += 1
                instruction.then_inc(router, 1)
                dve.wait_ge(router, count[0])

            def per_tile(v):
                return r_s[:, v, :].unsqueeze(2).broadcast_to([P, NT, NE])

            dve.wait_ge(logits_ready, 4)
            step(dve.reciprocal(r_s[:, 0, 0:1], temp[:]))
            step(dve.tensor_scalar(r_c[:], ps_u[:, 1, 0:NT * NE].rearrange("p (t e) -> p t e", e=NE), r_s[:, 0, 0:1], None, ALU.mult))
            step(dve.tensor_scalar(r_a[:], r_c[:], -80.0, None, ALU.max))
            dve.wait_ge(router_act, 1)
            step(dve.tensor_scalar(r_c[:], r_b[:], 1.0, None, ALU.add))
            step(dve.reciprocal(r_a[:], r_c[:]))
            step(dve.tensor_scalar(r_b[:], r_a[:], -CENTER, None, ALU.add))
            step(dve.scalar_tensor_tensor(r_c[:], r_b[:], -1.0, r_b[:], ALU.mult, ALU.max))
            step(dve.tensor_scalar(r_b[:], r_a[:], LOWER, None, ALU.is_ge))
            step(dve.scalar_tensor_tensor(r_wf[:], r_a[:], UPPER, r_b[:], ALU.is_le, ALU.mult))
            dve.wait_ge(router_act, 3)
            step(dve.tensor_tensor(r_b[:], r_w[:], r_wf[:], ALU.mult))
            step(dve.tensor_reduce(r_s[:, 1, :], r_b[:], AX_X, ALU.add))
            step(dve.tensor_scalar(r_s[:, 2, :], r_s[:, 1, :], 1e-8, None, ALU.is_lt))
            fb_j = r_fb[:].unsqueeze(2).broadcast_to([P, NT, NE, NE])
            fb_e = r_fb[:].unsqueeze(3).broadcast_to([P, NT, NE, NE])
            step(dve.tensor_tensor(r_gt[:], fb_j, fb_e, ALU.is_gt))
            step(dve.tensor_tensor(r_eq[:], fb_j, fb_e, ALU.is_equal))
            step(dve.tensor_tensor(r_eq[:], r_eq[:], tri[:].unsqueeze(1).broadcast_to([P, NT, NE, NE]), ALU.mult))
            step(dve.tensor_tensor(r_gt[:], r_gt[:], r_eq[:], ALU.add))
            step(dve.tensor_reduce(r_a[:], r_gt[:], AX_X, ALU.add))
            step(dve.scalar_tensor_tensor(r_c[:], r_a[:], 1.5, r_fb[:], ALU.is_lt, ALU.mult))
            step(dve.tensor_reduce(r_s[:, 3, :], r_c[:], AX_X, ALU.add))
            step(dve.tensor_scalar(r_s[:, 4, :], r_s[:, 3, :], 1e-8, None, ALU.max))
            step(dve.reciprocal(r_s[:, 5, :], r_s[:, 4, :]))
            step(dve.tensor_tensor(r_s[:, 6, :], r_s[:, 5, :], r_s[:, 2, :], ALU.mult))
            step(dve.tensor_tensor(r_a[:], r_c[:], per_tile(6), ALU.mult))
            step(dve.tensor_tensor(r_c[:], r_a[:], r_b[:], ALU.add))
            step(dve.tensor_reduce(r_s[:, 1, :], r_c[:], AX_X, ALU.add))
            step(dve.tensor_scalar(r_s[:, 3, :], r_s[:, 1, :], 1e-8, None, ALU.max))
            step(dve.reciprocal(r_s[:, 4, :], r_s[:, 3, :]))
            step(dve.tensor_tensor(r_wf[:], r_c[:], per_tile(4), ALU.mult))

            def split_e(e, par, from_sum):
                for m in range(3):
                    dve.wait_ge(we_hi_done, 3 * e + m + 1)
                    sl = slice(2 * m, 2 * m + 2)
                    src = we_f[:, e, sl, :] if from_sum else raw_e[:, par, sl, :]
                    dve.tensor_tensor(we_lo[:, par, sl, :], src, we_hi[:, par, sl, :], ALU.subtract).then_inc(we_split, 1)

            def product(m, f):
                dve.wait_ge(gu_ready, 4 * m + 2 * f + 2)
                dve.wait_ge(silu_done, 2 * m + f + 1)
                if later(due := 2 * m + f - 1):
                    dve.wait_ge(mid_split, due)
                dve.tensor_tensor(mid[:, f, :], ps_u[:, f, :], silu[:, f, :], ALU.mult).then_inc(mid_done, 1)

            def mid_tail(m, f, n):
                dve.wait_ge(mid_hi_done, 2 * m + f + 1)
                dve.tensor_tensor(mid_lo[:, n % 2, f, :], mid[:, f, :], mid_hi[:, n % 2, f, :], ALU.subtract).then_inc(mid_split, 1)

            def accumulate(m, par, n, finish):
                for t in range(4):
                    tt = 4 * n + t
                    dve.wait_ge(down_ready, 2 * m + t // 2 + 1)
                    if later(due := 4 * (m - 4) + t + 1):
                        dve.wait_ge(acc_done, due)
                    dve.scalar_tensor_tensor(acc[:, tt, :], ps_d[:, t // 2, (t % 2) * E:(t % 2 + 1) * E], wcol[:, par, tt:tt + 1],
                                             acc[:, tt, :], ALU.mult, ALU.add).then_inc(acc_done, 1)
                if finish:
                    for bb in range(2):
                        b = 2 * n + bb
                        sl = slice(4 * n + 2 * bb, 4 * n + 2 * bb + 2)
                        gb = gates[:, b, 1, :].unsqueeze(1).broadcast_to([P, TT, E])
                        dve.wait_ge(acc_done, 4 * m + 4)
                        dve.tensor_tensor(acc[:, sl, :], acc[:, sl, :], gb, ALU.mult).then_inc(final_mul, 1)
                    dve.wait_ge(final_mul, 2 * n + 2)
                    sl = slice(4 * n, 4 * n + 4)
                    dve.tensor_tensor(acc[:, sl, :], acc[:, sl, :], x_all[:, sl, :], ALU.add).then_inc(final_add, 1)

            def pair(j, first, last):
                for par in range(2):
                    e = 2 * j + par
                    if later(due := 16 * e - 16):
                        dve.wait_ge(acc_done, due)
                    dve.tensor_copy(wcol[:, par, :], r_wf[:, :, e]).then_inc(wcol_ready, 1)
                    for n in range(4):
                        m = 4 * e + n
                        product(m, 0)
                        product(m, 1)
                        if n:
                            accumulate(m - 1, par, n - 1, last and par == 1)
                        elif not (first and par == 0):
                            accumulate(m - 1, 1 - par, 3, False)
                        mid_tail(m, 0, n)
                        mid_tail(m, 1, n)
                        if n == 0:
                            dve.wait_ge(wcol_ready, e + 1)
                        if n == 1 and not (first and par == 0) and not (last and par == 1):
                            split_e(e + 1, 1 - par, False)

            split_e(0, 0, True)
            split_e(1, 1, True)
            dve.wait_ge(acc_zero, 1)
            pair(0, True, False)
            with dve.Fori(1, NE // 2 - 1) as j:
                pair(j, False, False)
            pair(NE // 2 - 1, False, True)
            accumulate(4 * NE - 1, 1, 3, True)

        @block.gpsimd
        def _(pool):
            pool.wait_ge(consts, 128)

            def inv_std(b):
                pool.wait_ge(ln_dve, 4 * b + 4)
                if later(due := 2 * b):
                    pool.wait_ge(ln_done, due)
                pool.tensor_tensor(veps[:], mv[:, :, 1], powers[:, 8:8 + TT], ALU.add).then_inc(veps_done, 1)
                pool.wait_ge(veps_done, b + 1)
                pool.tensor_tensor(rstd[:], veps[:], powers[:, 4:4 + TT], ALU.pow).then_inc(ln_rstd, 1)

            def unit(b, p):
                r = rot_of(p)
                pool.wait_ge(ssq_ready, NR * b + r + 1)
                if later(due := NR * b + r - 1):
                    pool.wait_ge(rnorm_ready, due)
                pool.tensor_tensor(root[:, r % 2, :], ssq[:, r % 2, :], powers[:, 0:4], ALU.pow).then_inc(root_ready, 1)
                pool.wait_ge(rotated, 3 * (NR * b + r + 1))
                pool.tensor_tensor(prod_c[:, r % 2], prod_c[:, r % 2], prod_s[:, r % 2], ALU.add).then_inc(rot_sum, 1)
                pool.wait_ge(rot_sum, NR * b + r + 1)
                pool.wait_ge(rnorm_ready, NR * b + r + 1)
                if later(due := NR * b + r + 1 - RING):
                    pool.wait_ge(rope_turned, due)
                pool.tensor_tensor(rows[:, r % RING], prod_c[:, r % 2], rnorm[:, r % 2, :].unsqueeze(2).broadcast_to([P, 4, D]),
                                   ALU.mult).then_inc(rows_ready, 1)

            def batch(b, last):
                for i in range(SLOTS):
                    for p in SLOT_PROJ[i]:
                        if p < NP:
                            if PROJ[p][0] != "v":
                                unit(b, p)
                        elif not last:
                            unit(b + 1, p - NP)
                    if i == 1 and not last:
                        inv_std(b + 1)

            inv_std(0)
            for p in range(LEAD):
                unit(0, p)
            batch(0, False)
            with pool.Fori(1, B - 1) as b:
                batch(b, False)
            batch(B - 1, True)

            pool.wait_ge(stage_a_done, 1)
            for n in range(4):
                pool.wait_ge(ln2_dve, 8 * n + 8)
                if later(due := 4 * n):
                    pool.wait_ge(ln2_done, due)
                pool.tensor_tensor(veps2[:], mv2[:, :, 1], powers[:, 8:12], ALU.add).then_inc(ln2_veps, 1)
                pool.wait_ge(ln2_veps, n + 1)
                pool.tensor_tensor(rstd2[:], veps2[:], powers[:, 4:8], ALU.pow).then_inc(ln2_rstd, 1)
                if n == 0:
                    pool.memset(acc[:], 0.0).then_inc(acc_zero, 1)


def tables():
    half = D // 2
    inv_freq = (np.float32(1.0) / np.float32(10000.0) ** (np.arange(half, dtype=np.float32) / np.float32(half))).astype(np.float32)
    ang = np.outer(np.arange(S, dtype=np.float32), inv_freq).astype(np.float32)
    ang = np.concatenate([ang, ang], axis=-1)
    cos, sin = np.cos(ang).astype(np.float32), np.sin(ang).astype(np.float32)
    sin[:, :half] *= -1.0
    pos = np.arange(S)
    win = (np.abs(pos[:, None] - pos[None, :]) <= WIN).astype(np.float32)
    cross = np.stack([win[0:P, P:S], win[P:S, 0:P]])
    mask = np.ascontiguousarray(np.broadcast_to(cross.transpose(1, 0, 2)[:, :, None, :], (P, 2, 2, P)))
    sel = np.zeros((B, B, P), np.float32)
    sel[np.arange(B), np.arange(B), :] = 1.0
    powers = np.empty((P, 12), np.float32)
    powers[:, :4], powers[:, 4:8], powers[:, 8:] = 0.5, -0.5, LN_EPS
    tri = np.ascontiguousarray(np.broadcast_to((np.arange(NE)[None, :] < np.arange(NE)[:, None]).astype(np.float32), (P, NE, NE)))
    return {
        "cos": np.ascontiguousarray(cos.reshape(TT, P, D).transpose(1, 0, 2)),
        "sin": np.ascontiguousarray(sin.reshape(TT, P, D).transpose(1, 0, 2)),
        "mask": mask, "sel": sel, "powers": powers, "tri": tri, "ident": np.eye(P, dtype=np.float32),
    }


def kernel(**inputs):
    import concourse.bacc as _bacc
    from concourse.bass_utils import run_bass_kernel_spmd as _run

    v = {k.removeprefix("L0_"): np.asarray(x) for k, x in inputs.items()}

    def tiles(m, width):
        return m.reshape(-1, P, width).transpose(1, 0, 2)

    wq, wk, wv = v["attn_wq"], v["attn_wk"], v["attn_wv"]
    blocks = {WK: wk, WV: wv}
    for g, c in enumerate(WQ):
        blocks[c] = wq[:, g * CHUNK:(g + 1) * CHUNK]
    arrays = {
        "x": tiles(v["attn_hidden_states"].reshape(B * S, E), E),
        "wqkv": np.stack([tiles(blocks[c], CHUNK) for c in range(CHUNKS)], axis=1),
        "wo": tiles(v["attn_wo"], E).reshape(P, 4, 4 * E),
        "wmod": tiles(v["wmod"], 6 * E),
        "cT": tiles(np.ascontiguousarray(v["c"].T), B),
        "qks": np.stack([v["attn_query_scale"], v["attn_key_scale"]], axis=1),
        "we": np.concatenate([v[f"ffn_{n}"].reshape(NE, KT, P, F).transpose(2, 0, 1, 3) for n in ("Wg", "Wu", "Wd")], axis=2),
        "lowA": np.stack([v[f"ffn_{n}"].transpose(2, 0, 1) for n in ("Ga", "Ua", "Da")], axis=2),
        "lowB": np.stack([v[f"ffn_{n}"].transpose(1, 0, 2) for n in ("Gb", "Ub", "Db")], axis=2),
        "wr": tiles(v["ffn_Wr"], NE),
        "temp": np.broadcast_to(v["ffn_temperature"].reshape(1, 1), (P, 1)),
    }
    arrays.update(tables())
    arrays = {f"in_{n}": np.ascontiguousarray(x) for n, x in arrays.items()}
    nc = _bacc.Bacc("TRN2", target_bir_lowering=False, num_devices=1)
    aps = {n[3:]: nc.dram_tensor(n, x.shape, mybir.dt.from_np(x.dtype), kind="ExternalInput").ap() for n, x in arrays.items()}
    out = nc.dram_tensor("out", (P, NT, E), F32, kind="ExternalOutput").ap()
    build(nc, aps, out)
    r = _run(nc, [arrays], core_ids=[0])
    return np.asarray(r.results[0]["out"]).transpose(1, 0, 2).reshape(B, S, E)
```

```python
from contextlib import ExitStack

import numpy as np

import concourse.bass as bass
from concourse import mybir

F32 = mybir.dt.float32
F32R = mybir.dt.float32r
ALU = mybir.AluOpType
ACT = mybir.ActivationFunctionType
AX_X = mybir.AxisListType.X

P = 128
B, S, E = 8, 256, 256
H, KV, D = 16, 4, 128
G = H // KV
WIN, CAP, EPS = 128, 50.0, 1e-6
LN_EPS = 1e-5
NE, F, R, NL = 8, 256, 64, 2
TT = S // P
KT = E // P
NT = B * TT
SLOTS = H // 2
QKV = (2 * KV + H) * D
CHUNK = 512
CHUNKS = QKV // CHUNK
CENTER = 1.0 / np.e
LOWER, UPPER = 0.5 - float(np.log(4.0 / 3.0)), 0.5
SCALE = 1.0 / float(np.sqrt(D)) / CAP

ORDER = (NL, *range(NL), *range(NL + 1, NE))

WK, WQ, WV = 0, (1, 2, 4, 5), 3

PROJ = [("k", 0, 0), ("k", 0, 1), ("q", 0, 0), ("q", 0, 1), ("q", 1, 0),
        ("q", 1, 1), ("v", 0, 0), ("v", 0, 1), ("q", 2, 0), ("q", 2, 1), ("q", 3, 0), ("q", 3, 1)]
LEAD = 6
NP = len(PROJ)
ROT = [u for u in PROJ if u[0] != "v"]
NR = len(ROT)
NQ = NR - TT
RING = 5
SLOT_PROJ = [[6, 7], [8], [9, 10], [11], [NP], [NP + 1, NP + 2], [NP + 3], [NP + 4, NP + 5]]
SLOT_TURN = [[4], [5], [6], [7], [8], [9, NR], [NR + 1, NR + 2], [NR + 3]]
LOADS = [("w", 0), ("w", 1), ("w", 2), ("w", 3), ("w", 4), ("o", 0), ("w", 5), ("o", 1), ("o", 2), ("o", 3)]
SLOT_SPLIT = [[4, 5], [6], [7], [], [8], [], [9], []]
RAW_RING = 3


def rot_of(p):
    return p if p < LEAD else p - TT


def build(nc, a, out):
    ctx = ExitStack()
    stage_a = ExitStack()

    def sb(name, shape, dt=F32, stack=ctx):
        return stack.enter_context(nc.sbuf_tensor(name, shape, dt))

    def ps(name, shape, stack=ctx):
        return stack.enter_context(nc.psum_tensor(name, shape, F32))

    def sem(name):
        return ctx.enter_context(nc.semaphore(name))

    with ctx:
        x_all = sb("x_all", [P, NT, E])
        modc = sb("modc", [P, B, 8])
        gates = sb("gates", [P, B, 2, E])
        ident = sb("ident", [P, P])
        powers = sb("powers", [P, 12])
        mv2 = sb("mv2", [P, NT, 2])
        veps2 = sb("veps2", [P, NT])
        rstd2 = sb("rstd2", [P, NT])
        raw_e = sb("raw_e", [P, 2, 6, F])

        def sba(name, shape, dt=F32):
            return sb(name, shape, dt, stage_a)

        w_hi = sba("w_hi", [P, CHUNKS, KT, CHUNK], F32R)
        w_lo = sba("w_lo", [P, CHUNKS, KT, CHUNK], F32R)
        wo_hi = sba("wo_hi", [P, H, E], F32R)
        wo_lo = sba("wo_lo", [P, H, E], F32R)
        cosT = sba("cosT", [P, TT, D])
        sinT = sba("sinT", [P, TT, D])
        mask = sba("mask", [P, 2, 2, P])
        kcol = sba("kcol", [P, 1])
        curmod = sba("curmod", [P, 4])
        stats2 = sba("stats2", [P, TT, 6])
        mv2b = sba("mv2b", [P, TT, 2])
        stats = sba("stats", [P, TT, 6])
        mv = sba("mv", [P, TT, 2])
        veps = sba("veps", [P, TT])
        rstd = sba("rstd", [P, TT])
        xn = sba("xn", [P, TT, E])
        hf = sba("hf", [P, KT, S])
        h_hi = sba("h_hi", [P, KT, S], F32R)
        h_lo = sba("h_lo", [P, KT, S], F32R)
        sq = sba("sq", [P, 4, D])
        prod_c = sba("prod_c", [P, 2, 4, D])
        prod_s = sba("prod_s", [P, 2, 4, D])
        ssq = sba("ssq", [P, 2, 4])
        root = sba("root", [P, 2, 4])
        roote = sba("roote", [P, 2, 4])
        rnorm = sba("rnorm", [P, 2, 4])
        rows = sba("rows", [P, RING, 4, D])
        kf = sba("kf", [P, TT, KV, P])
        kT_hi = sba("kT_hi", [P, TT, KV, P], F32R)
        kT_lo = sba("kT_lo", [P, TT, KV, P], F32R)
        qT_hi = sba("qT_hi", [P, 2, G, S], F32R)
        qT_lo = sba("qT_lo", [P, 2, G, S], F32R)
        vaug = sba("vaug", [P, TT, KV, D + 1])
        probs = sba("probs", [P, 2, 2 * 2 * S])
        rden = sba("rden", [P, TT, 2])
        o_rows = sba("o_rows", [P, TT, 2, D])
        oT_hi = sba("oT_hi", [P, TT, 2, P], F32R)
        oT_lo = sba("oT_lo", [P, TT, 2, P], F32R)
        ygated = sba("ygated", [P, TT, E])

        qks = sba("qks", [P, 2])
        spot = sba("spot", [P, 1])

        raw_w = raw_e[:].rearrange("p a m f -> p (a m f)").rearrange("p (r k n) -> p r k n", r=RAW_RING, k=KT)
        cT = kf[:, 0, 0, 0:KT * B].rearrange("p (k b) -> p k b", k=KT)
        scT = kf[:, 0, 1, 0:KT * B].rearrange("p (k b) -> p k b", k=KT)
        wmod_sb = x_all[:, TT:TT + 6 * KT, :].rearrange("p (k j) e -> p k (j e)", k=KT)
        spare = gates[:].rearrange("p b a e -> p (b a e)")
        grow, gabs, gsgn, gfin = (spare[0:B, n * 2 * E:(n + 1) * 2 * E] for n in range(4))
        gates_dram = nc.dram_tensor("gate_rows_dram", (B, 2 * E), F32, kind="Internal").ap()
        stage_a.close()

        h2_hi = sb("h2_hi", [P, KT, NT * P], F32R)
        h2_lo = sb("h2_lo", [P, KT, NT * P], F32R)
        h2f = sb("h2f", [P, 2, KT, 2 * S])
        x2n = sb("x2n", [P, 2, 4, E])
        r_log = sb("r_log", [P, NT, NE])
        wr = sb("wr", [P, KT, NE])
        lowA = sb("lowA", [R, NL, 3, E])
        lowB = sb("lowB", [R, NL, 3, E])
        we_hi = sb("we_hi", [P, 2, 6, F], F32R)
        we_lo = sb("we_lo", [P, 2, 6, F], F32R)
        we_f = sb("we_f", [P, NL, 6, F])
        temp = sb("temp", [P, 1])
        tri = sb("tri", [P, NE, NE])
        r_a = sb("r_a", [P, NT, NE])
        r_b = sb("r_b", [P, NT, NE])
        r_c = sb("r_c", [P, NT, NE])
        r_w = sb("r_w", [P, NT, NE])
        r_fb = sb("r_fb", [P, NT, NE])
        r_wf = sb("r_wf", [P, NT, NE])
        r_gt = sb("r_gt", [P, NT, NE, NE])
        r_eq = sb("r_eq", [P, NT, NE, NE])
        r_s = sb("r_s", [P, 8, NT])
        wcol = sb("wcol", [P, 2, NT])
        silu = sb("silu", [P, 2, 2 * S])
        mid = sb("mid", [P, 2, 2 * S])
        mid_hi = sb("mid_hi", [P, 2, 2, 2 * S], F32R)
        mid_lo = sb("mid_lo", [P, 2, 2, 2 * S], F32R)
        acc = sb("acc", [P, NT, E])

        psum_a = ExitStack()
        ps_proj = ps("ps_proj", [P, 2, 512], psum_a)
        ps_turn = ps("ps_turn", [P, 512], psum_a)
        ps_s = ps("ps_s", [P, 2, 512], psum_a)
        ps_o = ps("ps_o", [P, 2, 512], psum_a)
        ps_y = ps("ps_y", [P, 512], psum_a)
        psum_a.close()
        ps_g = ps("ps_g", [P, 2, 512])
        ps_u = ps("ps_u", [P, 2, 512])
        ps_d = ps("ps_d", [P, 2, 512])
        ps_t = ps("ps_t", [P, 2, 512])

        x_in = [sem("x_first"), sem("x_rest")]
        raw_in = [sem(f"raw_in{n}") for n in range(RAW_RING)]
        expert_in = [sem("expert_in0"), sem("expert_in1")]
        consts = sem("consts")
        wmod_in = sem("wmod_in")
        low_in = sem("low_in")
        out_done = sem("out_done")
        silu_c = sem("silu_c")
        mod_cols = sem("mod_cols")
        mod_rows = sem("mod_rows")
        gate_rows = sem("gate_rows")
        prologue_done = sem("prologue_done")
        w_hi_done = sem("w_hi_done")
        w_lo_done = sem("w_lo_done")
        ln_dve = sem("ln_dve")
        ln_rstd = sem("ln_rstd")
        ln_done = sem("ln_done")
        h_turned = sem("h_turned")
        h_done = sem("h_done")
        h_hi_done = sem("h_hi_done")
        h_split = sem("h_split")
        proj_ready = sem("proj_ready")
        square_ready = sem("square_ready")
        rotated = sem("rotated")
        ssq_ready = sem("ssq_ready")
        root_ready = sem("root_ready")
        rnorm_ready = sem("rnorm_ready")
        rot_sum = sem("rot_sum")
        rows_ready = sem("rows_ready")
        rope_turned = sem("rope_turned")
        k_scaled = sem("k_scaled")
        v_ready = sem("v_ready")
        scores_ready = sem("scores_ready")
        tanh_done = sem("tanh_done")
        exp_done = sem("exp_done")
        masked = sem("masked")
        pv_ready = sem("pv_ready")
        rden_done = sem("rden_done")
        o_rows_ready = sem("o_rows_ready")
        o_turned = sem("o_turned")
        o_hi = sem("o_hi")
        o_split = sem("o_split")
        y_ready = sem("y_ready")
        y_gated = sem("y_gated")
        x_updated = sem("x_updated")
        eps_added = sem("eps_added")
        veps_done = sem("veps_done")
        h_mod = sem("h_mod")
        mod_ready = sem("mod_ready")
        curmod_ready = sem("curmod_ready")
        ln2_rstd = sem("ln2_rstd")
        ln2_veps = sem("ln2_veps")
        ln2_done = sem("ln2_done")
        h2_turned = sem("h2_turned")
        h2_mod = sem("h2_mod")
        h2_hi_done = sem("h2_hi_done")
        h2_split = sem("h2_split")
        logits_ready = sem("logits_ready")
        router_act = sem("router_act")
        router = sem("router")
        low_ready = sem("low_ready")
        we_added = sem("we_added")
        we_hi_done = sem("we_hi_done")
        we_split = sem("we_split")
        gu_ready = sem("gu_ready")
        silu_done = sem("silu_done")
        mid_done = sem("mid_done")
        mid_hi_done = sem("mid_hi_done")
        mid_split = sem("mid_split")
        down_ready = sem("down_ready")
        acc_done = sem("acc_done")
        wcol_ready = sem("wcol_ready")
        final_mul = sem("final_mul")
        final_add = sem("final_add")
        acc_zero = sem("acc_zero")
        c_in = sem("c_in")
        wr_in = sem("wr_in")
        gates_out = sem("gates_out")
        gates_in = sem("gates_in")
        k_hi = sem("k_hi")
        q_hi = sem("q_hi")
        k_split = sem("k_split")
        q_split = sem("q_split")
        x2_stats = sem("x2_stats")
        x2_aggr = sem("x2_aggr")
        x2_kept = sem("x2_kept")
        logits_read = sem("logits_read")
        stage_a_done = sem("stage_a_done")

        def later(value):
            return not isinstance(value, int) or value > 0

        block = ctx.enter_context(nc.Block())

        @block.sync
        def _(sp):
            sp.dma_start(wmod_sb[:, :, 0:2 * E], a["wmod"][:, :, 0:2 * E]).then_inc(wmod_in, 16)
            sp.wait_ge(wmod_in, 16)
            for c, (kind, n) in enumerate(LOADS):
                if c >= RAW_RING:
                    sp.wait_ge(w_lo_done, c - RAW_RING + 1)
                src = a["wqkv"][:, n] if kind == "w" else a["wo"][:, n]
                sp.dma_start(raw_w[:, c % RAW_RING], src).then_inc(raw_in[c % RAW_RING], 16)
                if c == 0:
                    sp.dma_start(wmod_sb[:, :, 2 * E:], a["wmod"][:, :, 2 * E:]).then_inc(wmod_in, 16)
                if c == 3:
                    sp.wait_ge(gate_rows, 5)
                    sp.dma_start(gates_dram, gfin).then_inc(gates_out, 16)
                    sp.wait_ge(gates_out, 16)
                    sp.dma_start(gates[:].rearrange("p b a e -> p (b a e)"),
                                 gates_dram.rearrange("b n -> (b n)").unsqueeze(0).broadcast_to([P, B * 2 * E])).then_inc(gates_in, 16)
                    sp.dma_start(x_all[:, TT:NT, :], a["x"][:, TT:NT, :]).then_inc(x_in[1], 16)
            sp.wait_ge(w_lo_done, len(LOADS))
            for e in range(2):
                sp.dma_start(raw_e[:, e], a["we"][:, e]).then_inc(expert_in[e], 16)
            sp.wait_ge(stage_a_done, 1)
            sp.dma_start(wr[:], a["wr"]).then_inc(wr_in, 16)
            sp.dma_start(lowA[:], a["lowA"]).then_inc(low_in, 16)
            sp.dma_start(lowB[:], a["lowB"]).then_inc(low_in, 16)
            sp.dma_start(tri[:], a["tri"]).then_inc(low_in, 16)
            sp.dma_start(temp[:], a["temp"]).then_inc(low_in, 16)

            def load(e, par):
                sp.wait_ge(we_split, 3 * (e - 1))
                sp.dma_start(raw_e[:, par], a["we"][:, e]).then_inc(expert_in[par], 16)
            with sp.Fori(1, NE // 2) as j:
                load(2 * j, 0)
                load(2 * j + 1, 1)
            for n in range(4):
                sp.wait_ge(final_add, n + 1)
                sp.dma_start(out[:, 4 * n:4 * n + 4, :], acc[:, 4 * n:4 * n + 4, :]).then_inc(out_done, 16)
            sp.wait_ge(out_done, 64)

        @block.tensor
        def _(pe):
            def three(dst, hi, lo, w_h, w_l, first, last):
                pe.matmul(dst, hi, w_h, start=first, stop=False, skip_group_check=True)
                pe.matmul(dst, hi, w_l, start=False, stop=False, skip_group_check=True)
                return pe.matmul(dst, lo, w_h, start=False, stop=last, skip_group_check=True)

            def modulation_columns(dst, blocks):
                for j, block_of in enumerate(blocks):
                    for et in range(KT):
                        for k in range(KT):
                            at = block_of * E + et * P
                            mm = pe.matmul(dst[:, (2 * j + et) * B:(2 * j + et + 1) * B], wmod_sb[:, k, at:at + P],
                                           scT[:, k, :], start=(j == 0 and et == 0 and k == 0), stop=(k == KT - 1),
                                           skip_group_check=True)
                mm.then_inc(mod_cols, 1)

            def turn_h(b):
                if isinstance(b, int) and b == 0:
                    pe.wait_ge(consts, 96)
                else:
                    pe.wait_ge(q_split, NQ * b - 2)
                pe.wait_ge(ln_done, 2 * b + 2)
                for k in range(KT):
                    for t in range(TT):
                        mm = pe.transpose(ps_turn[:, k * S + t * P:k * S + (t + 1) * P], xn[:, t, k * P:(k + 1) * P], ident[:])
                mm.then_inc(h_turned, 1)

            def project(b, p):
                kind, g, t = PROJ[p]
                if p in (8, 9):
                    pe.wait_ge(v_ready, 2 * b + p - 7)
                elif later(due := NR * b + rot_of(p - 2) + 1 if p >= 2 else NR * b - 1 + p):
                    pe.wait_ge(ssq_ready, due)
                pe.wait_ge(h_split, b + 1)
                c = WK if kind == "k" else WV if kind == "v" else WQ[g]
                if isinstance(b, int) and b == 0:
                    pe.wait_ge(w_lo_done, LOADS.index(("w", c)) + 1)
                for k in range(KT):
                    mm = three(ps_proj[:, p % 2, :], h_hi[:, k, t * P:(t + 1) * P], h_lo[:, k, t * P:(t + 1) * P],
                               w_hi[:, c, k, :], w_lo[:, c, k, :], k == 0, k == KT - 1)
                mm.then_inc(proj_ready, 1)

            def turn_rows(b, r):
                if r == 0:
                    if isinstance(b, int) and b == 0:
                        pe.wait_ge(h_done, 1)
                    else:
                        pe.wait_ge(q_split, NQ * b)
                elif r == 1:
                    if isinstance(b, int) and b == 0:
                        pe.wait_ge(k_scaled, 1)
                    else:
                        pe.wait_ge(o_split, SLOTS * b - 2)
                elif r == 2:
                    pe.wait_ge(k_scaled, 2 * b + 2)
                elif r == 3:
                    if isinstance(b, int) and b == 0:
                        pe.wait_ge(q_split, 1)
                    else:
                        pe.wait_ge(o_split, SLOTS * b - 1)
                else:
                    if isinstance(b, int) and b == 0 and r == 4:
                        pe.wait_ge(q_split, 2)
                    else:
                        pe.wait_ge(o_split, SLOTS * b + r - 4)
                pe.wait_ge(rows_ready, NR * b + r + 1)
                for i in range(4):
                    mm = pe.transpose(ps_turn[:, i * P:(i + 1) * P], rows[:, r % RING, i, :], ident[:])
                mm.then_inc(rope_turned, 1)

            def turn_o(b, i, last):
                if i <= 2:
                    pe.wait_ge(q_split, NQ * b + 3 + i)
                elif i == 3:
                    pe.wait_ge(q_split, NQ * b + 6)
                    if not last:
                        pe.wait_ge(h_done, b + 2)
                elif i == 4:
                    pe.wait_ge(q_split, NQ * b + 7)
                elif i == 5 and not last:
                    pe.wait_ge(k_scaled, 2 * b + 3)
                elif i == 5:
                    pe.wait_ge(q_split, NQ * b + 8)
                elif i == 6 and not last:
                    pe.wait_ge(q_split, NQ * b + 9)
                else:
                    pe.wait_ge(o_split, SLOTS * b + i)
                pe.wait_ge(o_rows_ready, SLOTS * b + i + 1)
                for t in range(TT):
                    for h in range(2):
                        mm = pe.transpose(ps_turn[:, (2 * t + h) * P:(2 * t + h + 1) * P], o_rows[:, t, h, :], ident[:])
                mm.then_inc(o_turned, 1)

            def out_proj(b, i):
                pe.wait_ge(o_split, SLOTS * b + i + 1)
                pair = i % SLOTS
                if pair == 0 and later(b):
                    pe.wait_ge(y_gated, b)
                if isinstance(b, int) and b == 0:
                    pe.wait_ge(w_lo_done, LOADS.index(("o", pair // 2)) + 1)
                for t in range(TT):
                    for h in range(2):
                        mm = three(ps_y[:, t * E:(t + 1) * E], oT_hi[:, t, h, :], oT_lo[:, t, h, :],
                                   wo_hi[:, 2 * pair + h, :], wo_lo[:, 2 * pair + h, :],
                                   pair == 0 and t == 0 and h == 0, pair == SLOTS - 1 and h == 1)
                if pair == SLOTS - 1:
                    mm.then_inc(y_ready, 1)

            def scores(b, i):
                g, pair = i // 2, i % 2
                pe.wait_ge(q_split, NQ * b + 2 + 2 * g)
                if i == 0:
                    pe.wait_ge(k_split, 2 * b + 2)
                if later(due := SLOTS * b + i):
                    pe.wait_ge(exp_done, due)
                for t in range(TT):
                    q = slice(2 * pair, 2 * pair + 2)
                    mm = three(ps_s[:, t, :], kT_hi[:, t, g, :], kT_lo[:, t, g, :],
                               qT_hi[:, g % 2, q, :].rearrange("p h s -> p (h s)"),
                               qT_lo[:, g % 2, q, :].rearrange("p h s -> p (h s)"), True, True)
                mm.then_inc(scores_ready, 1)

            def weighted(b, i):
                g = i // 2
                pe.wait_ge(masked, SLOTS * b + i + 1)
                if later(due := SLOTS * b + i):
                    pe.wait_ge(o_rows_ready, due)
                if i == 0:
                    pe.wait_ge(v_ready, 2 * b + 2)
                for t in range(TT):
                    for h in range(2):
                        for k in range(TT):
                            at = (2 * k + h) * S + t * P
                            mm = pe.matmul(ps_o[:, t, h * (D + 1):(h + 1) * (D + 1)], probs[:, i % 2, at:at + P],
                                           vaug[:, k, g, :], start=(h == 0 and k == 0), stop=(k == TT - 1),
                                           skip_group_check=True)
                mm.then_inc(pv_ready, 1)

            def batch(b, first, last):
                for i in range(SLOTS):
                    scores(b, i)
                    if not (first and i == 0):
                        turn_o(b, i - 1, last)
                    for p in SLOT_PROJ[i]:
                        if p < NP:
                            project(b, p)
                        elif not last:
                            project(b + 1, p - NP)
                    if not (first and i == 0):
                        out_proj(b, i - 1)
                    for r in SLOT_TURN[i]:
                        if r < NR:
                            turn_rows(b, r)
                        elif not last:
                            turn_rows(b + 1, r - NR)
                    if i == 3 and not last:
                        turn_h(b + 1)
                    weighted(b, i)

            pe.wait_ge(silu_c, 1)
            pe.wait_ge(wmod_in, 16)
            modulation_columns(ps_s[:, 0, :], (0, 1))
            turn_h(0)
            for p in range(2):
                project(0, p)
            pe.wait_ge(wmod_in, 32)
            modulation_columns(ps_o[:, 0, :], (3, 4))
            for j, block_of in enumerate((2, 5)):
                for k in range(KT):
                    mm = pe.matmul(ps_s[0:B, 1, j * E:(j + 1) * E], scT[:, k, :],
                                   wmod_sb[:, k, block_of * E:(block_of + 1) * E],
                                   start=(j == 0 and k == 0), stop=(k == KT - 1), skip_group_check=True)
            mm.then_inc(mod_rows, 1)
            for p in range(2, 4):
                project(0, p)
            turn_rows(0, 0)
            turn_rows(0, 1)
            project(0, 4)
            turn_rows(0, 2)
            turn_rows(0, 3)
            project(0, 5)
            pe.wait_ge(gate_rows, 1)
            pe.wait_ge(mod_ready, 2)
            batch(0, True, False)
            with pe.Fori(1, B - 1) as b:
                batch(b, False, False)
            batch(B - 1, False, True)
            pe.wait_ge(o_split, SLOTS * B - 1)
            pe.wait_ge(o_rows_ready, SLOTS * B)
            for t in range(TT):
                for h in range(2):
                    mm = pe.transpose(ps_turn[:, (2 * t + h) * P:(2 * t + h + 1) * P], o_rows[:, t, h, :], ident[:])
            mm.then_inc(o_turned, 1)
            out_proj(B, -1)

            def turn_h2(n):
                pe.wait_ge(ln2_done, 4 * n + 4)
                if n >= 2:
                    pe.wait_ge(h2_mod, 4 * n - 4)
                for bb in range(2):
                    for k in range(KT):
                        for t in range(TT):
                            mm = pe.transpose((ps_t, ps_g)[n % 2][:, bb, k * S + t * P:k * S + (t + 1) * P],
                                              x2n[:, n % 2, 2 * bb + t, k * P:(k + 1) * P], ident[:])
                mm.then_inc(h2_turned, 1)

            def router_logits(n):
                pe.wait_ge(h2_mod, 4 * n + 4)
                if n == 0:
                    pe.wait_ge(wr_in, 16)
                for t in range(4):
                    for k in range(KT):
                        mm = pe.matmul(ps_u[:, 1, (4 * n + t) * NE:(4 * n + t + 1) * NE], h2f[:, n % 2, k, t * P:(t + 1) * P],
                                       wr[:, k, :], start=(n == 0 and t == 0 and k == 0), stop=(k == KT - 1),
                                       skip_group_check=True)
                mm.then_inc(logits_ready, 1)

            def low_rank(i):
                e, m = i // 3, i % 3
                if i == 0:
                    pe.wait_ge(low_in, 64)
                    pe.wait_ge(h2_mod, 16)
                if later(due := i - 1):
                    pe.wait_ge(we_added, due)
                for k in range(KT):
                    mm = pe.matmul(ps_t[:, i % 2, k * F:(k + 1) * F], lowA[:, e, m, k * P:(k + 1) * P], lowB[:, e, m, :],
                                   start=(k == 0), stop=True, skip_group_check=True)
                mm.then_inc(low_ready, 1)

            def gate_up(e, par, n):
                m = 4 * e + n
                if n == 0:
                    pe.wait_ge(we_split, 3 * e + 2)
                if isinstance(e, int) and e == 0:
                    pe.wait_ge(h2_split, n + 1)
                    if n == 0:
                        pe.wait_ge(logits_read, 1)
                for f in range(2):
                    if later(due := 2 * m + f - 1):
                        pe.wait_ge(mid_done, due)
                    for dst, w0 in ((ps_g, 0), (ps_u, 2)):
                        for k in range(KT):
                            mm = three(dst[:, f, :], we_hi[:, par, w0 + k, f * P:(f + 1) * P],
                                       we_lo[:, par, w0 + k, f * P:(f + 1) * P],
                                       h2_hi[:, k, n * 512:(n + 1) * 512], h2_lo[:, k, n * 512:(n + 1) * 512],
                                       k == 0, k == KT - 1)
                        mm.then_inc(gu_ready, 1)

            def down(e, par, n):
                m = 4 * e + n
                if n == 0:
                    pe.wait_ge(we_split, 3 * e + 3)
                pe.wait_ge(mid_split, 2 * m + 2)
                for half in range(2):
                    if later(due := 4 * m - 2 + 2 * half):
                        pe.wait_ge(acc_done, due)
                    for t in range(2):
                        tt = 2 * half + t
                        for f in range(2):
                            mm = three(ps_d[:, half, t * E:(t + 1) * E], mid_hi[:, n % 2, f, tt * P:(tt + 1) * P],
                                       mid_lo[:, n % 2, f, tt * P:(tt + 1) * P],
                                       we_hi[:, par, 4 + f, :], we_lo[:, par, 4 + f, :], t == 0 and f == 0, f == 1)
                    mm.then_inc(down_ready, 1)

            def pair(j, first):
                for par in range(2):
                    e = 2 * j + par
                    for n in range(4):
                        gate_up(e, par, n)
                        if n:
                            down(e, par, n - 1)
                        elif not (first and par == 0):
                            down(e - 1, 1 - par, 3)
                        if first and par == 0 and n == 2:
                            for i in range(3, 6):
                                low_rank(i)

            turn_h2(0)
            for n in range(1, 4):
                turn_h2(n)
                router_logits(n - 1)
            router_logits(3)
            for i in range(3):
                low_rank(i)
            pair(0, True)
            with pe.Fori(1, NE // 2 - 1) as j:
                pair(j, False)
            pair(NE // 2 - 1, False)
            down(NE - 1, 1, 3)

        @block.scalar
        def _(act):
            act.dma_start(cT, a["cT"]).then_inc(c_in, 16)
            act.dma_start(x_all[:, 0:TT, :], a["x"][:, 0:TT, :]).then_inc(x_in[0], 16)
            act.dma_start(powers[:], a["powers"]).then_inc(consts, 16)
            act.dma_start(ident[:], a["ident"]).then_inc(consts, 16)
            act.dma_start(cosT[:], a["cos"]).then_inc(consts, 16)
            act.dma_start(sinT[:], a["sin"]).then_inc(consts, 16)
            act.dma_start(qks[:], a["qks"]).then_inc(consts, 16)
            act.dma_start(mask[:], a["mask"]).then_inc(consts, 16)
            act.wait_ge(c_in, 16)
            act.activation(scT, cT, ACT.Silu).then_inc(silu_c, 1)

            def split_w(c):
                kind, n = LOADS[c]
                dst = w_hi[:, n] if kind == "w" else wo_hi[:, 4 * n:4 * n + 4, :].rearrange("p (k h) e -> p k (h e)", k=KT)
                act.wait_ge(raw_in[c % RAW_RING], 16 * (c // RAW_RING + 1))
                act.activation(dst, raw_w[:, c % RAW_RING], ACT.Copy).then_inc(w_hi_done, 1)

            def modulate(b):
                act.wait_ge(h_turned, b + 1)
                if later(b):
                    act.wait_ge(h_split, b)
                for k in range(KT):
                    act.activation(hf[:, k, :], ps_turn[:, k * S:(k + 1) * S], ACT.Identity,
                                   bias=curmod[:, k:k + 1], scale=curmod[:, 2 + k:3 + k]).then_inc(h_mod if k < KT - 1 else h_done, 1)
                act.wait_ge(h_mod, b + 1)
                act.wait_ge(h_done, b + 1)
                if later(due := NP * b):
                    act.wait_ge(proj_ready, due)
                act.activation(h_hi[:], hf[:], ACT.Copy).then_inc(h_hi_done, 1)

            def square(b, p):
                act.wait_ge(proj_ready, NP * b + p + 1)
                if PROJ[p][0] == "v":
                    t = PROJ[p][2]
                    if later(due := SLOTS * b):
                        act.wait_ge(pv_ready, due)
                    act.activation(vaug[:, t, :, 0:D], ps_proj[:, p % 2, :].rearrange("p (h d) -> p h d", h=KV),
                                   ACT.Copy).then_inc(v_ready, 1)
                else:
                    if later(due := NR * b + rot_of(p)):
                        act.wait_ge(ssq_ready, due)
                    act.activation(sq[:].rearrange("p h d -> p (h d)"), ps_proj[:, p % 2, :], ACT.Square).then_inc(square_ready, 1)

            def k_scale(b, r):
                act.wait_ge(rope_turned, NR * b + r + 1)
                if isinstance(b, int) and b == 0:
                    act.wait_ge(prologue_done, 2)
                if later(due := 2 * b):
                    act.wait_ge(k_split, due)
                act.activation(kf[:, r], ps_turn[:].rearrange("p (h q) -> p h q", h=4), ACT.Copy,
                               scale=kcol[:, 0:1]).then_inc(k_scaled, 1)

            def k_head(b, t):
                act.wait_ge(k_scaled, 2 * b + 2)
                if later(due := SLOTS * b):
                    act.wait_ge(scores_ready, due)
                act.activation(kT_hi[:, t], kf[:, t], ACT.Copy).then_inc(k_hi, 1)

            def q_head(b, r):
                kind, g, t = ROT[r]
                act.wait_ge(rope_turned, NR * b + r + 1)
                if later(due := SLOTS * b + 2 * g - 2 if g >= 2 else SLOTS * (b - 1) + 2 * g + 6):
                    act.wait_ge(scores_ready, due)
                act.activation(qT_hi[:, g % 2, :, t * P:(t + 1) * P], ps_turn[:].rearrange("p (h q) -> p h q", h=4),
                               ACT.Copy).then_inc(q_hi, 1)

            def soft(b, i):
                act.wait_ge(scores_ready, SLOTS * b + i + 1)
                act.activation(ps_s[:], ps_s[:], ACT.Tanh).then_inc(tanh_done, 1)

            def expo(b, i):
                act.wait_ge(tanh_done, SLOTS * b + i + 1)
                if later(due := SLOTS * b + i - 1):
                    act.wait_ge(pv_ready, due)
                act.activation(probs[:, i % 2, :], ps_s[:].rearrange("p k n -> p (k n)"), ACT.Exp, scale=CAP).then_inc(exp_done, 1)

            def o_head(b, i):
                act.wait_ge(o_turned, SLOTS * b + i + 1)
                act.activation(oT_hi[:].rearrange("p t h q -> p (t h q)"), ps_turn[:], ACT.Copy).then_inc(o_hi, 1)

            def turned(b, r):
                if ROT[r][0] == "k":
                    k_scale(b, r)
                else:
                    q_head(b, r)

            def batch(b, first, last):
                for i in range(SLOTS):
                    soft(b, i)
                    if not (first and i == 0):
                        o_head(b, i - 1)
                    expo(b, i)
                    for p in SLOT_PROJ[i]:
                        if p < NP:
                            square(b, p)
                        elif not last:
                            square(b + 1, p - NP)
                    for r in SLOT_TURN[i]:
                        if r < NR:
                            turned(b, r)
                        elif not last:
                            turned(b + 1, r - NR)
                    if i == 3 and not last:
                        modulate(b + 1)
                    if i == 7 and not last:
                        k_head(b + 1, 0)
                        k_head(b + 1, 1)
                    if first:
                        for c in SLOT_SPLIT[i]:
                            split_w(c)

            def columns(n, src):
                cols = src[:, 0:4 * B].rearrange("p (j b) -> p b j", b=B)
                act.wait_ge(mod_cols, n + 1)
                act.activation(modc[:, :, 4 * n:4 * n + 2], cols[:, :, 0:2], ACT.Copy)
                act.activation(modc[:, :, 4 * n + 2:4 * n + 4], cols[:, :, 2:4], ACT.Copy, bias=1.0).then_inc(mod_ready, 1)

            columns(0, ps_s[:, 0, :])
            modulate(0)
            split_w(0)
            square(0, 0)
            square(0, 1)
            columns(1, ps_o[:, 0, :])
            split_w(1)
            square(0, 2)
            square(0, 3)
            k_scale(0, 0)
            k_scale(0, 1)
            split_w(2)
            square(0, 4)
            k_head(0, 0)
            k_head(0, 1)
            q_head(0, 2)
            q_head(0, 3)
            square(0, 5)
            split_w(3)
            batch(0, True, False)
            with act.Fori(1, B - 1) as b:
                batch(b, False, False)
            batch(B - 1, False, True)
            o_head(B, -1)

            act.wait_ge(stage_a_done, 1)

            def modulate2(n):
                act.wait_ge(h2_turned, n + 1)
                if n >= 2:
                    act.wait_ge(h2_split, n - 1)
                    act.wait_ge(logits_ready, n - 1)
                for bb in range(2):
                    for k in range(KT):
                        act.activation(h2f[:, n % 2, k, bb * S:(bb + 1) * S], (ps_t, ps_g)[n % 2][:, bb, k * S:(k + 1) * S],
                                       ACT.Identity, bias=modc[:, 2 * n + bb, 4 + k:5 + k],
                                       scale=modc[:, 2 * n + bb, 6 + k:7 + k]).then_inc(h2_mod, 1)
                act.wait_ge(h2_mod, 4 * n + 4)
                act.activation(h2_hi[:, :, n * 512:(n + 1) * 512], h2f[:, n % 2], ACT.Copy).then_inc(h2_hi_done, 1)

            def split_e(e, par, low=None):
                for m in range(3):
                    if low is None:
                        act.wait_ge(expert_in[par], 8 * e + 16 - 8 * par)
                    else:
                        act.wait_ge(we_added, 3 * low + m + 1)
                    if later(due := 16 * (e - 1) if m < 2 else 8 * (e - 1)):
                        act.wait_ge(gu_ready if m < 2 else down_ready, due)
                    sl = slice(2 * m, 2 * m + 2)
                    src = raw_e[:, par, sl, :] if low is None else we_f[:, low, sl, :]
                    act.activation(we_hi[:, par, sl, :], src, ACT.Copy).then_inc(we_hi_done, 1)

            def silu_of(m, f):
                act.wait_ge(gu_ready, 4 * m + 2 * f + 1)
                if later(due := 2 * m + f - 1):
                    act.wait_ge(mid_done, due)
                act.activation(silu[:, f, :], ps_g[:, f, :], ACT.Silu).then_inc(silu_done, 1)

            def mid_head(m, f, n):
                act.wait_ge(mid_done, 2 * m + f + 1)
                if later(due := 2 * (m - 1)):
                    act.wait_ge(down_ready, due)
                act.activation(mid_hi[:, n % 2, f, :], mid[:, f, :], ACT.Copy).then_inc(mid_hi_done, 1)

            def pair(j, first, last):
                for par in range(2):
                    e = 2 * j + par
                    for n in range(4):
                        m = 4 * e + n
                        silu_of(m, 0)
                        silu_of(m, 1)
                        mid_head(m, 0, n)
                        mid_head(m, 1, n)
                        if first and par == 0 and n == 1:
                            act.wait_ge(router, 3)
                            act.activation(r_b[:], r_a[:], ACT.Exp, scale=-1.0).then_inc(router_act, 1)
                            act.wait_ge(router, 9)
                            act.activation(r_w[:], r_c[:], ACT.Exp, scale=-1.0 / 0.1).then_inc(router_act, 1)
                            act.activation(r_fb[:], r_c[:], ACT.Exp, scale=-1.0 / 0.3).then_inc(router_act, 1)
                        if n == 2 and not (last and par == 1):
                            split_e(e + 1, 1 - par, par if first else None)

            for n in range(4):
                modulate2(n)
            split_e(0, 0)
            pair(0, True, False)
            with act.Fori(1, NE // 2 - 1) as j:
                pair(j, False, False)
            pair(NE // 2 - 1, False, True)

        @block.vector
        def _(dve):
            def norm_stats(b):
                dve.wait_ge(x_in[0] if isinstance(b, int) and b == 0 else x_in[1], 16)
                if later(b):
                    dve.wait_ge(ln_rstd, b)
                for t in range(TT):
                    dve.bn_stats(stats[:, t, :], x_all[:, TT * b + t, :]).then_inc(ln_dve, 1)
                if later(b):
                    dve.wait_ge(h_done, b)
                    if later(due := 2 * (b - 1)):
                        dve.wait_ge(x2_stats, due)
                else:
                    dve.wait_ge(mod_ready, 1)
                dve.wait_ge(ln_dve, 4 * b + 2)
                dve.tensor_copy(curmod[:], modc[:, b, 0:4]).then_inc(curmod_ready, 1)
                for t in range(TT):
                    dve.bn_aggr(mv[:, t, :], stats[:, t, :]).then_inc(ln_dve, 1)

            def norm_rows(b):
                dve.wait_ge(ln_rstd, b + 1)
                if later(b):
                    dve.wait_ge(h_turned, b)
                for t in range(TT):
                    dve.tensor_scalar(xn[:, t, :], x_all[:, TT * b + t, :], mv[:, t, 0:1], rstd[:, t:t + 1],
                                      ALU.subtract, ALU.mult).then_inc(ln_done, 1)

            def split_w(c):
                kind, n = LOADS[c]
                lo, hi = (w_lo[:, n], w_hi[:, n]) if kind == "w" else (
                    v[:, 4 * n:4 * n + 4, :].rearrange("p (k h) e -> p k (h e)", k=KT) for v in (wo_lo, wo_hi))
                dve.wait_ge(w_hi_done, c + 1)
                dve.tensor_tensor(lo, raw_w[:, c % RAW_RING], hi, ALU.subtract).then_inc(w_lo_done, 1)

            def h_tail(b):
                dve.wait_ge(h_hi_done, b + 1)
                dve.tensor_tensor(h_lo[:], hf[:], h_hi[:], ALU.subtract).then_inc(h_split, 1)

            def rotate(b, p):
                r = rot_of(p)
                t = PROJ[p][2]
                src = ps_proj[:, p % 2, :].rearrange("p (h d) -> p h d", h=4)
                cs = cosT[:, t, :].unsqueeze(1).broadcast_to([P, 4, D])
                dve.wait_ge(square_ready, NR * b + r + 1)
                if later(due := NR * b + r - 1):
                    dve.wait_ge(rows_ready, due)
                dve.tensor_tensor(prod_c[:, r % 2], src, cs, ALU.mult).then_inc(rotated, 1)
                for half in range(2):
                    o = half * D // 2
                    other = D // 2 - o
                    sn = sinT[:, t, o:o + D // 2].unsqueeze(1).broadcast_to([P, 4, D // 2])
                    dve.tensor_tensor(prod_s[:, r % 2, :, o:o + D // 2], src[:, :, other:other + D // 2], sn,
                                      ALU.mult).then_inc(rotated, 1)
                dve.tensor_reduce(ssq[:, r % 2, :], sq[:], AX_X, ALU.add).then_inc(ssq_ready, 1)

            def inverse(b, p):
                r = rot_of(p)
                dve.wait_ge(root_ready, NR * b + r + 1)
                dve.tensor_scalar(roote[:, r % 2, :], root[:, r % 2, :], EPS, None, ALU.add).then_inc(eps_added, 1)
                dve.wait_ge(eps_added, NR * b + r + 1)
                dve.reciprocal(rnorm[:, r % 2, :], roote[:, r % 2, :]).then_inc(rnorm_ready, 1)

            def k_tail(b, t):
                dve.wait_ge(k_hi, 2 * b + t + 1)
                dve.tensor_tensor(kT_lo[:, t], kf[:, t], kT_hi[:, t], ALU.subtract).then_inc(k_split, 1)

            def q_tail(b, r):
                kind, g, t = ROT[r]
                q = slice(t * P, (t + 1) * P)
                dve.wait_ge(q_hi, NQ * b + r - 1)
                dve.tensor_tensor(qT_lo[:, g % 2, :, q], ps_turn[:].rearrange("p (h q) -> p h q", h=4),
                                  qT_hi[:, g % 2, :, q], ALU.subtract).then_inc(q_split, 1)

            def apply_mask(b, i):
                pm = probs[:, i % 2, P:7 * P].rearrange("p (k s c) -> p k s c", k=2, s=3)[:, :, 0:3:2, :]
                dve.wait_ge(exp_done, SLOTS * b + i + 1)
                dve.tensor_tensor(pm, pm, mask[:], ALU.mult).then_inc(masked, 1)

            def normalise(b, i):
                o = ps_o[:, :, 0:2 * (D + 1)].rearrange("p t (h d) -> p t h d", h=2)
                dve.wait_ge(pv_ready, SLOTS * b + i + 1)
                dve.reciprocal(rden[:], o[:, :, :, D]).then_inc(rden_done, 1)
                dve.wait_ge(rden_done, SLOTS * b + i + 1)
                if later(due := SLOTS * b + i):
                    dve.wait_ge(o_turned, due)
                dve.tensor_tensor(o_rows[:], o[:, :, :, 0:D], rden[:].unsqueeze(3).broadcast_to([P, TT, 2, D]),
                                  ALU.mult).then_inc(o_rows_ready, 1)

            def o_tail(b, i):
                dve.wait_ge(o_hi, SLOTS * b + i + 1)
                dve.tensor_tensor(oT_lo[:].rearrange("p t h q -> p (t h q)"), ps_turn[:],
                                  oT_hi[:].rearrange("p t h q -> p (t h q)"), ALU.subtract).then_inc(o_split, 1)

            def residual(b):
                if isinstance(b, int) and b == 0:
                    dve.wait_ge(gates_in, 16)
                dve.wait_ge(y_ready, b + 1)
                ga = gates[:, b, 0, :].unsqueeze(1).broadcast_to([P, TT, E])
                dve.tensor_tensor(ygated[:], ps_y[:].rearrange("p (t e) -> p t e", t=TT), ga, ALU.mult).then_inc(y_gated, 1)
                dve.wait_ge(y_gated, b + 1)
                xb = x_all[:, bass.ds(TT * b, TT), :]
                dve.tensor_tensor(xb, xb, ygated[:], ALU.add).then_inc(x_updated, 1)
                dve.wait_ge(x_updated, b + 1)
                if later(b):
                    dve.wait_ge(x2_aggr, 2 * b)
                dve.tensor_copy(spot[:], kcol[:])
                for t in range(TT):
                    dve.bn_stats(stats2[:, t, :], x_all[:, TT * b + t, :]).then_inc(x2_stats, 1)

            def aggregate(b):
                if isinstance(b, int):
                    dve.wait_ge(x2_stats, 2 * b + 2)
                    if later(b):
                        dve.wait_ge(x2_kept, b)
                for t in range(TT):
                    dve.bn_aggr(mv2b[:, t, :], stats2[:, t, :]).then_inc(x2_aggr, 1)
                dve.wait_ge(x2_aggr, 2 * b + 2)
                dve.tensor_copy(mv2[:, bass.ds(TT * b, TT), :], mv2b[:]).then_inc(x2_kept, 1)

            def batch(b, first, last):
                for i in range(SLOTS):
                    units = [(b, p) if p < NP else (b + 1, p - NP) for p in SLOT_PROJ[i] if p < NP or not last]
                    units = [(bb, p) for bb, p in units if PROJ[p][0] != "v"]
                    if not (first and i == 0):
                        o_tail(b, i - 1)
                    apply_mask(b, i)
                    for bb, p in units:
                        rotate(bb, p)
                    for r in SLOT_TURN[i]:
                        if 2 <= r < NR:
                            q_tail(b, r)
                        elif r >= NR + 2 and not last:
                            q_tail(b + 1, r - NR)
                    if i == 7 and not last:
                        k_tail(b + 1, 0)
                        k_tail(b + 1, 1)
                    normalise(b, i)
                    for bb, p in units:
                        inverse(bb, p)
                    if i == 0 and not first:
                        residual(b - 1)
                    if i == 1:
                        if not last:
                            norm_stats(b + 1)
                        if not first:
                            aggregate(b - 1)
                    if i == 2 and not last:
                        norm_rows(b + 1)
                    if i == 3 and not last:
                        h_tail(b + 1)
                    if first:
                        for c in SLOT_SPLIT[i]:
                            split_w(c)

            norm_stats(0)
            norm_rows(0)
            dve.wait_ge(consts, 96)
            dve.scalar_tensor_tensor(kcol[:], qks[:, 0:1], SCALE, qks[:, 1:2], ALU.mult, ALU.mult).then_inc(prologue_done, 1)
            dve.memset(vaug[:, :, :, D:D + 1], 1.0).then_inc(prologue_done, 1)
            h_tail(0)
            split_w(0)
            rotate(0, 0)
            rotate(0, 1)
            inverse(0, 0)
            split_w(1)
            inverse(0, 1)
            dve.wait_ge(mod_rows, 1)
            dve.tensor_copy(grow, ps_s[0:B, 1, :]).then_inc(gate_rows, 1)
            dve.wait_ge(gate_rows, 1)
            dve.scalar_tensor_tensor(gabs, grow, -1.0, grow, ALU.mult, ALU.max).then_inc(gate_rows, 1)
            dve.tensor_scalar(gsgn, grow, 0.0, 2.0, ALU.is_ge, ALU.mult).then_inc(gate_rows, 1)
            dve.wait_ge(gate_rows, 3)
            dve.tensor_scalar(gsgn, gsgn, -1.0, None, ALU.add).then_inc(gate_rows, 1)
            dve.wait_ge(gate_rows, 4)
            dve.scalar_tensor_tensor(gfin, gabs, 0.25, gsgn, ALU.max, ALU.mult).then_inc(gate_rows, 1)
            rotate(0, 2)
            rotate(0, 3)
            inverse(0, 2)
            split_w(2)
            inverse(0, 3)
            rotate(0, 4)
            inverse(0, 4)
            k_tail(0, 0)
            k_tail(0, 1)
            q_tail(0, 2)
            q_tail(0, 3)
            rotate(0, 5)
            inverse(0, 5)
            split_w(3)
            batch(0, True, False)
            with dve.Fori(1, B - 1) as b:
                batch(b, False, False)
            batch(B - 1, False, True)
            o_tail(B, -1)
            residual(B - 1)
            aggregate(B - 1)
            dve.wait_ge(x2_kept, B)
            dve.memset(ygated[:, 0, 0:1], 0.0).then_inc(stage_a_done, 1)

            def h2_tail(n):
                m = slice(n * 512, (n + 1) * 512)
                dve.wait_ge(h2_hi_done, n + 1)
                dve.tensor_tensor(h2_lo[:, :, m], h2f[:, n % 2], h2_hi[:, :, m], ALU.subtract).then_inc(h2_split, 1)

            def fold(low, e):
                for m3 in range(3):
                    i = 3 * low + m3
                    sl = slice(2 * m3, 2 * m3 + 2)
                    dve.wait_ge(expert_in[e % 2], 16 * (e // 2 + 1))
                    dve.wait_ge(low_ready, i + 1)
                    dve.tensor_tensor(we_f[:, low, sl, :], ps_t[:, i % 2, :].rearrange("p (k f) -> p k f", k=2),
                                      raw_e[:, e % 2, sl, :], ALU.add).then_inc(we_added, 1)

            def route():
                count = [0]

                def step(instruction):
                    count[0] += 1
                    instruction.then_inc(router, 1)
                    dve.wait_ge(router, count[0])

                def per_tile(v):
                    return r_s[:, v, :].unsqueeze(2).broadcast_to([P, NT, NE])

                step(dve.reciprocal(r_s[:, 0, 0:1], temp[:]))
                step(dve.tensor_scalar(r_c[:], r_log[:], r_s[:, 0, 0:1], None, ALU.mult))
                step(dve.tensor_scalar(r_a[:], r_c[:], -80.0, None, ALU.max))
                dve.wait_ge(router_act, 1)
                step(dve.tensor_scalar(r_c[:], r_b[:], 1.0, None, ALU.add))
                step(dve.reciprocal(r_a[:], r_c[:]))
                step(dve.tensor_scalar(r_b[:], r_a[:], -CENTER, None, ALU.add))
                step(dve.scalar_tensor_tensor(r_c[:], r_b[:], -1.0, r_b[:], ALU.mult, ALU.max))
                step(dve.tensor_scalar(r_b[:], r_a[:], LOWER, None, ALU.is_ge))
                step(dve.scalar_tensor_tensor(r_wf[:], r_a[:], UPPER, r_b[:], ALU.is_le, ALU.mult))
                dve.wait_ge(router_act, 3)
                step(dve.tensor_tensor(r_b[:], r_w[:], r_wf[:], ALU.mult))
                step(dve.tensor_reduce(r_s[:, 1, :], r_b[:], AX_X, ALU.add))
                step(dve.tensor_scalar(r_s[:, 2, :], r_s[:, 1, :], 1e-8, None, ALU.is_lt))
                fb_j = r_fb[:].unsqueeze(2).broadcast_to([P, NT, NE, NE])
                fb_e = r_fb[:].unsqueeze(3).broadcast_to([P, NT, NE, NE])
                step(dve.tensor_tensor(r_gt[:], fb_j, fb_e, ALU.is_gt))
                step(dve.tensor_tensor(r_eq[:], fb_j, fb_e, ALU.is_equal))
                step(dve.tensor_tensor(r_eq[:], r_eq[:], tri[:].unsqueeze(1).broadcast_to([P, NT, NE, NE]), ALU.mult))
                step(dve.tensor_tensor(r_gt[:], r_gt[:], r_eq[:], ALU.add))
                step(dve.tensor_reduce(r_a[:], r_gt[:], AX_X, ALU.add))
                step(dve.scalar_tensor_tensor(r_c[:], r_a[:], 1.5, r_fb[:], ALU.is_lt, ALU.mult))
                step(dve.tensor_reduce(r_s[:, 3, :], r_c[:], AX_X, ALU.add))
                step(dve.tensor_scalar(r_s[:, 4, :], r_s[:, 3, :], 1e-8, None, ALU.max))
                step(dve.reciprocal(r_s[:, 5, :], r_s[:, 4, :]))
                step(dve.tensor_tensor(r_s[:, 6, :], r_s[:, 5, :], r_s[:, 2, :], ALU.mult))
                step(dve.tensor_tensor(r_a[:], r_c[:], per_tile(6), ALU.mult))
                step(dve.tensor_tensor(r_c[:], r_a[:], r_b[:], ALU.add))
                step(dve.tensor_reduce(r_s[:, 1, :], r_c[:], AX_X, ALU.add))
                step(dve.tensor_scalar(r_s[:, 3, :], r_s[:, 1, :], 1e-8, None, ALU.max))
                step(dve.reciprocal(r_s[:, 4, :], r_s[:, 3, :]))
                step(dve.tensor_tensor(r_wf[:], r_c[:], per_tile(4), ALU.mult))

            def split_e(e, par, low=None):
                for m in range(3):
                    sl = slice(2 * m, 2 * m + 2)
                    src = raw_e[:, par, sl, :] if low is None else we_f[:, low, sl, :]
                    dve.wait_ge(we_hi_done, 3 * e + m + 1)
                    dve.tensor_tensor(we_lo[:, par, sl, :], src, we_hi[:, par, sl, :], ALU.subtract).then_inc(we_split, 1)

            def product(m, f):
                dve.wait_ge(gu_ready, 4 * m + 2 * f + 2)
                dve.wait_ge(silu_done, 2 * m + f + 1)
                if later(due := 2 * m + f - 1):
                    dve.wait_ge(mid_split, due)
                dve.tensor_tensor(mid[:, f, :], ps_u[:, f, :], silu[:, f, :], ALU.mult).then_inc(mid_done, 1)

            def mid_tail(m, f, n):
                dve.wait_ge(mid_hi_done, 2 * m + f + 1)
                dve.tensor_tensor(mid_lo[:, n % 2, f, :], mid[:, f, :], mid_hi[:, n % 2, f, :], ALU.subtract).then_inc(mid_split, 1)

            def weights_of(e, par):
                if later(due := 16 * e - 16):
                    dve.wait_ge(acc_done, due)
                dve.tensor_copy(wcol[:, par, :], r_wf[:, :, e]).then_inc(wcol_ready, 1)

            def accumulate(m, par, n, finish=False):
                for t in range(4):
                    tt = 4 * n + t
                    dve.wait_ge(down_ready, 2 * m + t // 2 + 1)
                    if later(due := 4 * (m - 4) + t + 1):
                        dve.wait_ge(acc_done, due)
                    dve.scalar_tensor_tensor(acc[:, tt, :], ps_d[:, t // 2, (t % 2) * E:(t % 2 + 1) * E], wcol[:, par, tt:tt + 1],
                                             acc[:, tt, :], ALU.mult, ALU.add).then_inc(acc_done, 1)
                if finish:
                    dve.wait_ge(acc_done, 4 * m + 4)
                    for bb in range(2):
                        b = 2 * n + bb
                        sl = slice(4 * n + 2 * bb, 4 * n + 2 * bb + 2)
                        gb = gates[:, b, 1, :].unsqueeze(1).broadcast_to([P, TT, E])
                        dve.tensor_tensor(acc[:, sl, :], acc[:, sl, :], gb, ALU.mult).then_inc(final_mul, 1)
                    sl = slice(4 * n, 4 * n + 4)
                    dve.wait_ge(final_mul, 2 * n + 2)
                    dve.tensor_tensor(acc[:, sl, :], acc[:, sl, :], x_all[:, sl, :], ALU.add).then_inc(final_add, 1)

            def pair(j, first, last):
                for par in range(2):
                    e = 2 * j + par
                    for n in range(4):
                        m = 4 * e + n
                        product(m, 0)
                        product(m, 1)
                        mid_tail(m, 0, n)
                        mid_tail(m, 1, n)
                        if n == 0 and not (first and par == 0):
                            weights_of(e, par)
                        if n == 1 and first and par == 0:
                            route()
                            weights_of(0, 0)
                        if n == 1:
                            dve.wait_ge(wcol_ready, e + 1)
                        if n:
                            accumulate(m - 1, par, n - 1, last and par == 1)
                        elif not (first and par == 0):
                            accumulate(m - 1, 1 - par, 3)
                        if n == 2 and not (last and par == 1):
                            split_e(e + 1, 1 - par, par if first else None)
                        if first and par == 0 and n == 2:
                            fold(1, 2)

            dve.wait_ge(ln2_rstd, 2)
            for n in range(4):
                if n >= 2:
                    dve.wait_ge(h2_turned, n - 1)
                for t in range(4):
                    dve.tensor_scalar(x2n[:, n % 2, t, :], x_all[:, 4 * n + t, :], mv2[:, 4 * n + t, 0:1],
                                      rstd2[:, 4 * n + t:4 * n + t + 1], ALU.subtract, ALU.mult).then_inc(ln2_done, 1)
                if n:
                    h2_tail(n - 1)
            h2_tail(3)
            dve.wait_ge(logits_ready, 4)
            dve.tensor_copy(r_log[:], ps_u[:, 1, 0:NT * NE].rearrange("p (t e) -> p t e", e=NE)).then_inc(logits_read, 1)
            split_e(0, 0)
            fold(0, 1)
            dve.wait_ge(acc_zero, 1)
            dve.wait_ge(logits_read, 1)
            pair(0, True, False)
            with dve.Fori(1, NE // 2 - 1) as j:
                pair(j, False, False)
            pair(NE // 2 - 1, False, True)
            accumulate(4 * NE - 1, 1, 3, True)

        @block.gpsimd
        def _(pool):
            def inv_std(b):
                pool.wait_ge(ln_dve, 4 * b + 4)
                if later(due := 2 * b):
                    pool.wait_ge(ln_done, due)
                pool.tensor_tensor(veps[:], mv[:, :, 1], powers[:, 8:8 + TT], ALU.add).then_inc(veps_done, 1)
                pool.wait_ge(veps_done, b + 1)
                pool.tensor_tensor(rstd[:], veps[:], powers[:, 4:4 + TT], ALU.pow).then_inc(ln_rstd, 1)

            def root_and_sum(b, p):
                r = rot_of(p)
                pool.wait_ge(ssq_ready, NR * b + r + 1)
                if later(due := NR * b + r - 1):
                    pool.wait_ge(rnorm_ready, due)
                pool.tensor_tensor(root[:, r % 2, :], ssq[:, r % 2, :], powers[:, 0:4], ALU.pow).then_inc(root_ready, 1)
                pool.wait_ge(rotated, 3 * (NR * b + r + 1))
                pool.tensor_tensor(prod_c[:, r % 2], prod_c[:, r % 2], prod_s[:, r % 2], ALU.add).then_inc(rot_sum, 1)

            def unit_rows(b, p):
                r = rot_of(p)
                pool.wait_ge(rot_sum, NR * b + r + 1)
                pool.wait_ge(rnorm_ready, NR * b + r + 1)
                if later(due := NR * b + r + 1 - RING):
                    pool.wait_ge(rope_turned, due)
                pool.tensor_tensor(rows[:, r % RING], prod_c[:, r % 2], rnorm[:, r % 2, :].unsqueeze(2).broadcast_to([P, 4, D]),
                                   ALU.mult).then_inc(rows_ready, 1)

            def batch(b, last):
                for i in range(SLOTS):
                    units = [(b, p) if p < NP else (b + 1, p - NP) for p in SLOT_PROJ[i] if p < NP or not last]
                    units = [(bb, p) for bb, p in units if PROJ[p][0] != "v"]
                    for bb, p in units:
                        root_and_sum(bb, p)
                    if i == 1 and not last:
                        inv_std(b + 1)
                    for bb, p in units:
                        unit_rows(bb, p)

            pool.wait_ge(consts, 96)
            inv_std(0)
            root_and_sum(0, 0)
            for p in range(1, LEAD):
                root_and_sum(0, p)
                unit_rows(0, p - 1)
            unit_rows(0, LEAD - 1)
            batch(0, False)
            with pool.Fori(1, B - 1) as b:
                batch(b, False)
            batch(B - 1, True)

            for part, ready in ((slice(0, NT - TT), B - 1), (slice(NT - TT, NT), B)):
                n = part.stop - part.start
                pool.wait_ge(x2_kept, ready)
                pool.tensor_tensor(veps2[:, part], mv2[:, part, 1], powers[:, 8:9].broadcast_to([P, n]), ALU.add).then_inc(ln2_veps, 1)
                pool.wait_ge(ln2_veps, 1 if n > TT else 2)
                pool.tensor_tensor(rstd2[:, part], veps2[:, part], powers[:, 4:5].broadcast_to([P, n]), ALU.pow).then_inc(ln2_rstd, 1)
            pool.wait_ge(stage_a_done, 1)
            pool.memset(acc[:], 0.0).then_inc(acc_zero, 1)


def tables():
    half = D // 2
    inv_freq = (np.float32(1.0) / np.float32(10000.0) ** (np.arange(half, dtype=np.float32) / np.float32(half))).astype(np.float32)
    ang = np.outer(np.arange(S, dtype=np.float32), inv_freq).astype(np.float32)
    ang = np.concatenate([ang, ang], axis=-1)
    cos, sin = np.cos(ang).astype(np.float32), np.sin(ang).astype(np.float32)
    sin[:, :half] *= -1.0
    pos = np.arange(S)
    win = (np.abs(pos[:, None] - pos[None, :]) <= WIN).astype(np.float32)
    cross = np.stack([win[0:P, P:S], win[P:S, 0:P]])
    mask = np.ascontiguousarray(np.broadcast_to(cross.transpose(1, 0, 2)[:, :, None, :], (P, 2, 2, P)))
    powers = np.empty((P, 12), np.float32)
    powers[:, :4], powers[:, 4:8], powers[:, 8:] = 0.5, -0.5, LN_EPS
    number = np.array(ORDER)
    tri = np.ascontiguousarray(np.broadcast_to((number[None, :] < number[:, None]).astype(np.float32), (P, NE, NE)))
    return {
        "cos": np.ascontiguousarray(cos.reshape(TT, P, D).transpose(1, 0, 2)),
        "sin": np.ascontiguousarray(sin.reshape(TT, P, D).transpose(1, 0, 2)),
        "mask": mask, "powers": powers, "tri": tri, "ident": np.eye(P, dtype=np.float32),
    }


def kernel(**inputs):
    import concourse.bacc as _bacc
    from concourse.bass_utils import run_bass_kernel_spmd as _run

    v = {k.removeprefix("L0_"): np.asarray(x) for k, x in inputs.items()}

    def tiles(m, width):
        return m.reshape(-1, P, width).transpose(1, 0, 2)

    wq, wk, wv = v["attn_wq"], v["attn_wk"], v["attn_wv"]
    blocks = {WK: wk, WV: wv}
    for g, c in enumerate(WQ):
        blocks[c] = wq[:, g * CHUNK:(g + 1) * CHUNK]
    arrays = {
        "x": tiles(v["attn_hidden_states"].reshape(B * S, E), E),
        "wqkv": np.stack([tiles(blocks[c], CHUNK) for c in range(CHUNKS)], axis=1),
        "wo": tiles(v["attn_wo"], E).reshape(P, 4, KT, 2 * E),
        "wmod": tiles(v["wmod"], 6 * E),
        "cT": tiles(np.ascontiguousarray(v["c"].T), B),
        "qks": np.stack([v["attn_query_scale"], v["attn_key_scale"]], axis=1),
        "we": np.concatenate([v[f"ffn_{n}"][list(ORDER)].reshape(NE, KT, P, F).transpose(2, 0, 1, 3) for n in ("Wg", "Wu", "Wd")], axis=2),
        "lowA": np.stack([v[f"ffn_{n}"].transpose(2, 0, 1) for n in ("Ga", "Ua", "Da")], axis=2),
        "lowB": np.stack([v[f"ffn_{n}"].transpose(1, 0, 2) for n in ("Gb", "Ub", "Db")], axis=2),
        "wr": tiles(v["ffn_Wr"][:, list(ORDER)], NE),
        "temp": np.broadcast_to(v["ffn_temperature"].reshape(1, 1), (P, 1)),
    }
    arrays.update(tables())
    arrays = {f"in_{n}": np.ascontiguousarray(x) for n, x in arrays.items()}
    nc = _bacc.Bacc("TRN2", target_bir_lowering=False, num_devices=1)
    aps = {n[3:]: nc.dram_tensor(n, x.shape, mybir.dt.from_np(x.dtype), kind="ExternalInput").ap() for n, x in arrays.items()}
    out = nc.dram_tensor("out", (P, NT, E), F32, kind="ExternalOutput").ap()
    build(nc, aps, out)
    r = _run(nc, [arrays], core_ids=[0])
    return np.asarray(r.results[0]["out"]).transpose(1, 0, 2).reshape(B, S, E)
```
